# Optimizing a Trainium2 kernel written in Bass

```python
import numpy as np
import jax
import jax.numpy as jnp

def _softmax(x, axis=-1):
    return jax.nn.softmax(x, axis=axis)

def _gelu(x):
    return jax.nn.gelu(x, approximate=True)

def _silu(x):
    return jax.nn.silu(x)

def _sigmoid(x):
    return jax.nn.sigmoid(x)

def _layernorm(x, axis=-1, eps=1e-05):
    m = jnp.mean(x, axis=axis, keepdims=True)
    v = jnp.var(x, axis=axis, keepdims=True)
    return (x - m) / jnp.sqrt(v + eps)

def _scatter_add(tgt, idx, src, axis=0):
    return tgt.at[idx].add(src)

def _segment_sum(src, seg, n):
    return jax.ops.segment_sum(src, seg, n)
kernel_name = 'mk_vit_tower_d2_tok_img512_r4_d4e901'

def setup_inputs(seed: int=0):
    np.random.seed(seed)
    _w = jnp.asarray

    def _rec_inputs():
        import jax
        import jax.numpy as jnp
        _rk = jax.random.key(seed)
        x = -0.000477451 + 1.00034 * jax.random.normal(jax.random.fold_in(_rk, 1), (8, 32, 32, 29), jnp.float32)
        return x
    x = _rec_inputs()

    def _L0_tok_setup():
        import jax, jax.numpy as jnp
        import numpy as np
        import math
        H, W_DIM, D_MODEL, B = (32, 32, 128, 128)
        F_TOTAL = 29
        SEQ_LEN = H * W_DIM

        def make_pe(seq_len: int, d_model: int) -> jnp.ndarray:
            position = np.arange(seq_len, dtype=np.float32)[:, None]
            div_term = np.exp(np.arange(0, d_model, 2, dtype=np.float32) * (-math.log(10000.0) / d_model))
            pe = np.zeros((seq_len, d_model), dtype=np.float32)
            pe[:, 0::2] = np.sin(position * div_term)
            pe[:, 1::2] = np.cos(position * div_term)
            return jnp.asarray(pe)
        key = jax.random.key(seed)
        k1, k2 = jax.random.split(key)
        state_tensor = jax.random.normal(k1, (B, H, W_DIM, F_TOTAL), dtype=jnp.float32)
        W = jax.random.normal(k2, (F_TOTAL, D_MODEL), dtype=jnp.float32) * 0.05
        return {'state_tensor': state_tensor, 'W': W}
    _L0_tok_all = _L0_tok_setup()
    _L0_tok_in = {k: v for k, v in _L0_tok_all.items() if k in ('W',)}
    del _L0_tok_all

    def _L0_attn_setup():
        import jax, jax.numpy as jnp
        import numpy as np
        SIZE = 128
        NUM_HEADS = 8
        HEAD_SIZE = SIZE // NUM_HEADS
        EPS = 1e-05

        def _retention(x, W_Q, W_K, W_V):
            B, T, D = x.shape
            H, dh = (NUM_HEADS, HEAD_SIZE)
            q = (x @ W_Q).reshape(B, T, H, dh).transpose(0, 2, 1, 3)
            k = (x @ W_K).reshape(B, T, H, dh).transpose(0, 2, 1, 3)
            v = (x @ W_V).reshape(B, T, H, dh).transpose(0, 2, 1, 3)
            gammas = 1.0 - jnp.exp2(-5.0 - jnp.arange(H, dtype=jnp.float32))
            idx = jnp.arange(T)
            diff = (idx[:, None] - idx[None, :]).astype(jnp.float32)
            causal = diff >= 0
            decay = jnp.where(causal[None], jnp.exp(diff[None] * jnp.log(gammas)[:, None, None]), 0.0)
            scores = jnp.einsum('bhtd,bhsd->bhts', q, k) / jnp.sqrt(jnp.float32(dh))
            out = jnp.einsum('bhts,bhsd->bhtd', scores * decay[None], v)
            return out.transpose(0, 2, 1, 3).reshape(B, T, D)

        def _group_norm(y, weight, bias):
            B, T, D = y.shape
            g = y.reshape(B * T, NUM_HEADS, HEAD_SIZE)
            mean = jnp.mean(g, axis=-1, keepdims=True)
            var = jnp.var(g, axis=-1, keepdims=True)
            g = (g - mean) / jnp.sqrt(var + EPS)
            g = g.reshape(B * T, D) * weight + bias
            return g.reshape(B, T, D)
        key = jax.random.key(seed)
        ks = jax.random.split(key, 8)
        B, T, D = (2, 512, SIZE)
        mk = lambda k: jax.random.normal(k, (D, D), dtype=jnp.float32) / D
        return {'x': jax.random.normal(ks[0], (B, T, D), dtype=jnp.float32), 'W_Q': mk(ks[1]), 'W_K': mk(ks[2]), 'W_V': mk(ks[3]), 'W_G': mk(ks[4]), 'W_O': mk(ks[5]), 'gn_weight': jnp.ones((D,), dtype=jnp.float32), 'gn_bias': jnp.zeros((D,), dtype=jnp.float32)}
    _L0_attn_all = _L0_attn_setup()
    _L0_attn_in = {k: v for k, v in _L0_attn_all.items() if k in ('W_Q', 'W_K', 'W_V', 'W_G', 'W_O', 'gn_weight', 'gn_bias')}
    del _L0_attn_all

    def _L0_ffn_setup():
        import jax, jax.numpy as jnp
        import numpy as np
        EPS = 1e-09
        LN_EPS = 1e-05

        def _layernorm(x, gamma):
            x = x.astype(jnp.float32)
            mu = jnp.mean(x, axis=-1, keepdims=True)
            var = jnp.var(x, axis=-1, keepdims=True)
            return (x - mu) * jax.lax.rsqrt(var + LN_EPS) * gamma
        key = jax.random.key(seed)
        ks = jax.random.split(key, 5)
        b, n, d, e, h = (4, 256, 128, 6, 512)
        x = jax.random.normal(ks[0], (b, n, d), dtype=jnp.float32)
        w_gating = jax.random.normal(ks[1], (d, e), dtype=jnp.float32)
        std1 = 1.0 / np.sqrt(h)
        std2 = 1.0 / np.sqrt(d)
        w1 = jax.random.uniform(ks[2], (e, d, h), jnp.float32, -std1, std1)
        w2 = jax.random.uniform(ks[3], (e, h, d), jnp.float32, -std2, std2)
        gamma = jnp.ones((d,), dtype=jnp.float32)
        return {'x': x, 'w_gating': w_gating, 'gamma': gamma, 'w1': w1, 'w2': w2}
    _L0_ffn_all = _L0_ffn_setup()
    _L0_ffn_in = {k: v for k, v in _L0_ffn_all.items() if k in ('w_gating', 'gamma', 'w1', 'w2')}
    del _L0_ffn_all

    def _L1_attn_setup():
        import jax, jax.numpy as jnp
        import numpy as np
        HIDDEN_DIM = 64
        D = HIDDEN_DIM * 2
        key = jax.random.key(seed)
        ks = jax.random.split(key, 7)
        s = 1.0 / np.sqrt(D)
        x = jax.random.normal(ks[0], (8, 512, D), dtype=jnp.float32)
        Wq = jax.random.uniform(ks[1], (D, D), jnp.float32, -s, s)
        bq = jax.random.uniform(ks[2], (D,), jnp.float32, -s, s)
        Wk = jax.random.uniform(ks[3], (D, D), jnp.float32, -s, s)
        bk = jax.random.uniform(ks[4], (D,), jnp.float32, -s, s)
        Wv = jax.random.uniform(ks[5], (D, D), jnp.float32, -s, s)
        bv = jax.random.uniform(ks[6], (D,), jnp.float32, -s, s)
        return {'x': x, 'Wq': Wq, 'bq': bq, 'Wk': Wk, 'bk': bk, 'Wv': Wv, 'bv': bv}
    _L1_attn_all = _L1_attn_setup()
    _L1_attn_in = {k: v for k, v in _L1_attn_all.items() if k in ('Wq', 'bq', 'Wk', 'bk', 'Wv', 'bv')}
    del _L1_attn_all

    def _L1_ffn_setup():
        import jax, jax.numpy as jnp
        import numpy as np
        B, S, D, E, O = (256, 64, 128, 16, 128)
        key = jax.random.key(seed)
        k_x, k_wg, k_bg, k_we, k_be = jax.random.split(key, 5)
        scale_g = 1.0 / np.sqrt(D)
        scale_e = 1.0 / np.sqrt(D)
        return {'x': jax.random.normal(k_x, (B, S, D), dtype=jnp.float32), 'Wg': jax.random.uniform(k_wg, (D, E), jnp.float32, -scale_g, scale_g), 'bg': jax.random.uniform(k_bg, (E,), jnp.float32, -scale_g, scale_g), 'We': jax.random.uniform(k_we, (E, D, O), jnp.float32, -scale_e, scale_e), 'be': jax.random.uniform(k_be, (E, O), jnp.float32, -scale_e, scale_e)}
    _L1_ffn_all = _L1_ffn_setup()
    _L1_ffn_in = {k: v for k, v in _L1_ffn_all.items() if k in ('Wg', 'bg', 'We', 'be')}
    del _L1_ffn_all
    return {'x': x, 'L0_tok_W': _L0_tok_in['W'], 'L0_attn_W_Q': _L0_attn_in['W_Q'], 'L0_attn_W_K': _L0_attn_in['W_K'], 'L0_attn_W_V': _L0_attn_in['W_V'], 'L0_attn_W_G': _L0_attn_in['W_G'], 'L0_attn_W_O': _L0_attn_in['W_O'], 'L0_attn_gn_weight': _L0_attn_in['gn_weight'], 'L0_attn_gn_bias': _L0_attn_in['gn_bias'], 'L0_ffn_w_gating': _L0_ffn_in['w_gating'], 'L0_ffn_gamma': _L0_ffn_in['gamma'], 'L0_ffn_w1': _L0_ffn_in['w1'], 'L0_ffn_w2': _L0_ffn_in['w2'], 'L1_attn_Wq': _L1_attn_in['Wq'], 'L1_attn_bq': _L1_attn_in['bq'], 'L1_attn_Wk': _L1_attn_in['Wk'], 'L1_attn_bk': _L1_attn_in['bk'], 'L1_attn_Wv': _L1_attn_in['Wv'], 'L1_attn_bv': _L1_attn_in['bv'], 'L1_ffn_Wg': _L1_ffn_in['Wg'], 'L1_ffn_bg': _L1_ffn_in['bg'], 'L1_ffn_We': _L1_ffn_in['We'], 'L1_ffn_be': _L1_ffn_in['be']}

def reference(x, L0_tok_W, L0_attn_W_Q, L0_attn_W_K, L0_attn_W_V, L0_attn_W_G, L0_attn_W_O, L0_attn_gn_weight, L0_attn_gn_bias, L0_ffn_w_gating, L0_ffn_gamma, L0_ffn_w1, L0_ffn_w2, L1_attn_Wq, L1_attn_bq, L1_attn_Wk, L1_attn_bk, L1_attn_Wv, L1_attn_bv, L1_ffn_Wg, L1_ffn_bg, L1_ffn_We, L1_ffn_be):
    import jax
    import jax.numpy as jnp

    def _L0_tok_ref(state_tensor, W):
        import jax, jax.numpy as jnp
        import numpy as np
        import math
        H, W_DIM, D_MODEL, B = (32, 32, 128, 128)
        F_TOTAL = 29
        SEQ_LEN = H * W_DIM

        def make_pe(seq_len: int, d_model: int) -> jnp.ndarray:
            position = np.arange(seq_len, dtype=np.float32)[:, None]
            div_term = np.exp(np.arange(0, d_model, 2, dtype=np.float32) * (-math.log(10000.0) / d_model))
            pe = np.zeros((seq_len, d_model), dtype=np.float32)
            pe[:, 0::2] = np.sin(position * div_term)
            pe[:, 1::2] = np.cos(position * div_term)
            return jnp.asarray(pe)
        b, h, w, f = state_tensor.shape
        s = h * w
        x = state_tensor.reshape(b, s, f)
        emb = jnp.einsum('bsf,fd->bsd', x, W)
        pe = make_pe(s * 2, W.shape[1])[:s]
        return emb + pe[None, :, :]

    def _L0_attn_ref(x, W_Q, W_K, W_V, W_G, W_O, gn_weight, gn_bias):
        import jax, jax.numpy as jnp
        import numpy as np
        SIZE = 128
        NUM_HEADS = 8
        HEAD_SIZE = SIZE // NUM_HEADS
        EPS = 1e-05

        def _retention(x, W_Q, W_K, W_V):
            B, T, D = x.shape
            H, dh = (NUM_HEADS, HEAD_SIZE)
            q = (x @ W_Q).reshape(B, T, H, dh).transpose(0, 2, 1, 3)
            k = (x @ W_K).reshape(B, T, H, dh).transpose(0, 2, 1, 3)
            v = (x @ W_V).reshape(B, T, H, dh).transpose(0, 2, 1, 3)
            gammas = 1.0 - jnp.exp2(-5.0 - jnp.arange(H, dtype=jnp.float32))
            idx = jnp.arange(T)
            diff = (idx[:, None] - idx[None, :]).astype(jnp.float32)
            causal = diff >= 0
            decay = jnp.where(causal[None], jnp.exp(diff[None] * jnp.log(gammas)[:, None, None]), 0.0)
            scores = jnp.einsum('bhtd,bhsd->bhts', q, k) / jnp.sqrt(jnp.float32(dh))
            out = jnp.einsum('bhts,bhsd->bhtd', scores * decay[None], v)
            return out.transpose(0, 2, 1, 3).reshape(B, T, D)

        def _group_norm(y, weight, bias):
            B, T, D = y.shape
            g = y.reshape(B * T, NUM_HEADS, HEAD_SIZE)
            mean = jnp.mean(g, axis=-1, keepdims=True)
            var = jnp.var(g, axis=-1, keepdims=True)
            g = (g - mean) / jnp.sqrt(var + EPS)
            g = g.reshape(B * T, D) * weight + bias
            return g.reshape(B, T, D)
        ret = _retention(x, W_Q, W_K, W_V)
        normed = _group_norm(ret, gn_weight, gn_bias)
        return jax.nn.silu(x @ W_G + normed) @ W_O

    def _L0_ffn_ref(x, w_gating, gamma, w1, w2):
        import jax, jax.numpy as jnp
        import numpy as np
        EPS = 1e-09
        LN_EPS = 1e-05

        def _layernorm(x, gamma):
            x = x.astype(jnp.float32)
            mu = jnp.mean(x, axis=-1, keepdims=True)
            var = jnp.var(x, axis=-1, keepdims=True)
            return (x - mu) * jax.lax.rsqrt(var + LN_EPS) * gamma
        b, n, d = x.shape
        E = w_gating.shape[-1]
        C = max(min(n, int(n * 6.0 / E)), 4)
        raw = jnp.einsum('bnd,de->bne', x, w_gating)
        probs = jax.nn.softmax(raw, axis=-1)
        gate1 = jnp.max(probs, axis=-1)
        idx1 = jnp.argmax(probs, axis=-1)
        mask1 = jax.nn.one_hot(idx1, E, dtype=jnp.float32)
        gates_wo1 = probs * (1.0 - mask1)
        gate2 = jnp.max(gates_wo1, axis=-1)
        denom = gate1 + gate2 + EPS
        gate1 = gate1 / denom
        pos1 = (jnp.cumsum(mask1, axis=-2) - mask1) * mask1
        mask1 = mask1 * (pos1 < float(C)).astype(jnp.float32)
        mask1_flat = jnp.sum(mask1, axis=-1)
        pos1_flat = jnp.sum(pos1, axis=-1).astype(jnp.int32)
        gate1 = gate1 * mask1_flat
        combine = gate1[..., None, None] * mask1_flat[..., None, None] * jax.nn.one_hot(idx1, E, dtype=jnp.float32)[..., None] * jax.nn.one_hot(pos1_flat, C, dtype=jnp.float32)[..., None, :]
        dispatch = (combine != 0).astype(jnp.float32)
        expert_in = jnp.einsum('bnd,bnec->ebcd', x, dispatch)
        xn = _layernorm(expert_in, gamma)
        hidden = jax.nn.gelu(jnp.einsum('ebcd,edh->ebch', xn, w1), approximate=False)
        expert_out = jnp.einsum('ebch,ehd->ebcd', hidden, w2)
        out = jnp.einsum('ebcd,bnec->bnd', expert_out, combine)
        return out

    def _L1_attn_ref(x, Wq, bq, Wk, bk, Wv, bv):
        import jax, jax.numpy as jnp
        import numpy as np
        HIDDEN_DIM = 64
        D = HIDDEN_DIM * 2
        q = jnp.einsum('bnd,ed->bne', x, Wq) + bq
        k = jnp.einsum('bnd,ed->bne', x, Wk) + bk
        v = jnp.einsum('bnd,ed->bne', x, Wv) + bv
        scale = jnp.sqrt(jnp.float32(q.shape[-1])) + 1e-06
        scores = jnp.einsum('bqd,bkd->bqk', q, k) / scale
        attn = jax.nn.softmax(scores, axis=1)
        out = jnp.einsum('bqk,bkd->bqd', attn, v)
        return out

    def _L1_ffn_ref(x, Wg, bg, We, be):
        import jax, jax.numpy as jnp
        import numpy as np
        B, S, D, E, O = (256, 64, 128, 16, 128)
        scores = jax.nn.softmax(jnp.mean(x, axis=1) @ Wg + bg, axis=-1)
        idx = jnp.argmax(scores, axis=-1)
        gate = jnp.take_along_axis(scores, idx[:, None], axis=-1)
        W_sel = We[idx]
        b_sel = be[idx]
        y = jnp.einsum('bsd,bdo->bso', x, W_sel) + b_sel[:, None, :]
        return gate[:, :, None] * y
    h = _L0_tok_ref(x, L0_tok_W)
    h = h + _L0_attn_ref(_layernorm(h, axis=-1), L0_attn_W_Q, L0_attn_W_K, L0_attn_W_V, L0_attn_W_G, L0_attn_W_O, L0_attn_gn_weight, L0_attn_gn_bias)
    h = h + _L0_ffn_ref(_layernorm(h, axis=-1), L0_ffn_w_gating, L0_ffn_gamma, L0_ffn_w1, L0_ffn_w2)
    h = h + _L1_attn_ref(_layernorm(h, axis=-1), L1_attn_Wq, L1_attn_bq, L1_attn_Wk, L1_attn_bk, L1_attn_Wv, L1_attn_bv)
    h = h + _L1_ffn_ref(_layernorm(h, axis=-1), L1_ffn_Wg, L1_ffn_bg, L1_ffn_We, L1_ffn_be)
    return h

_drawn_inputs = setup_inputs


def setup_inputs(seed=0):
    import zlib

    import numpy as np

    out = dict(_drawn_inputs(seed))
    spreads = {'L0_attn_gn_weight': (1.0, 0.6),
     'L0_attn_gn_bias': (0.0, 0.607),
     'L0_ffn_gamma': (1.0, 0.2)}
    factors = {'L0_attn_W_G': 4.62,
     'L1_attn_bq': 64.0,
     'L1_attn_bk': 5.925,
     'L1_ffn_bg': 64.0,
     'L1_ffn_be': 7.822}
    for name, (base, spread) in spreads.items():
        noise = np.random.default_rng([zlib.crc32(name.encode()), seed]).standard_normal(out[name].shape)
        drawn = base * np.exp(spread * noise) if base else spread * noise
        out[name] = jnp.asarray(drawn.astype(out[name].dtype))
    for name, factor in factors.items():
        out[name] = (out[name] * factor).astype(out[name].dtype)
    return out
```

```python
import math
from contextlib import ExitStack

import numpy as np

import concourse.bass as bass
from concourse import mybir
from concourse.alu_op_type import AluOpType as ALU

ACT = mybir.ActivationFunctionType
F32 = mybir.dt.float32
BF16 = mybir.dt.bfloat16
I32 = mybir.dt.int32
U32 = mybir.dt.uint32
AXX = mybir.AxisListType.X

P = 128
B, SEQ, F_IN = 8, 1024, 29
TPB = SEQ // P
TILES = B * TPB
GT = 4
GROUPS = TILES // GT
GN = GT * P
H, DH = 8, 16
FX = GT * F_IN
E0, HID = 6, 512
HB = HID // P
ET = 256
NET = 38
E1 = 16
LP = 96
LN_EPS = 1e-5
GATE_EPS = 1e-9
SCALE1 = float(1.0 / (np.sqrt(np.float32(P)) + np.float32(1e-6)))
LN_EXP = "natural_log_exp_and_others"
NO_EXPERT = -3e38
CAP = TILES * P + ET
SPARE = NET - TILES * P // ET
ROWS = E0 * CAP + SPARE * ET
N_EXPERT = 2 * E0 + 1
N_FIRST = GT + 2
N_CONST = 21
POS0 = GT * LP
assert NET * ET >= TILES * P + (E0 - 1) * (ET - 1)
assert POS0 + (GT + 1) * E0 <= 512


def constants():
    pos = np.arange(SEQ, dtype=np.float32)[:, None]
    div = np.exp(np.arange(0, P, 2, dtype=np.float32) * (-math.log(10000.0) / P))
    pe = np.zeros((SEQ, P), np.float32)
    pe[:, 0::2] = np.sin(pos * div)
    pe[:, 1::2] = np.cos(pos * div)
    gam = 1.0 - np.exp2(-5.0 - np.arange(H, dtype=np.float64))
    t = np.arange(P)
    diff = t[None, :] - t[:, None]
    head = np.arange(P) // DH
    same = (head[:, None] == head[None, :]).astype(np.float64)
    dec = np.where(diff[:, None, :] >= 0, gam[None, :, None] ** np.maximum(diff, 0)[:, None, :], 0.0)
    out = {
        "pe": pe.reshape(TPB, P, P).transpose(1, 0, 2),
        "decay": dec / math.sqrt(DH),
        "q_decay": gam[head][:, None] ** (t[None, :] + 1) / math.sqrt(DH),
        "k_decay": gam[head][None, :] ** (P - 1 - t[:, None]),
        "state_decay": (gam[head] ** P)[:, None],
        "head_mask": (head[:, None] == np.arange(H)[None, :]),
        "same_head": same,
        "center": np.eye(P) - same / DH,
        "average": same / DH,
        "ident": np.eye(P),
        "before": t[:, None] < t[None, :],
        "expert_no": np.broadcast_to(np.arange(E0)[None, :], (P, E0)),
        "tile_no": np.broadcast_to(np.arange(NET)[None, :], (P, NET)),
        "region": np.broadcast_to(CAP * np.arange(E0)[None, :], (P, E0)),
    }
    return {k: np.ascontiguousarray(v, dtype=np.float32) for k, v in out.items()}


def above_zero(count):
    return not isinstance(count, int) or count > 0


def pipeline(eng, first, last, body_from, body_pairs, step):
    for n in range(first, body_from):
        step(n, n // 2, n % 2, n)
    with eng.Fori(0, body_pairs) as k:
        step(2 * k + body_from, k + body_from // 2, 0, None)
        step(2 * k + body_from + 1, k + body_from // 2, 1, None)
    for n in range(body_from + 2 * body_pairs, last + 1):
        step(n, n // 2, n % 2, n)


class Shared:
    pass


def tower(nc, t, cst, out):
    with ExitStack() as ctx:
        def sb(name, shape, dt=F32):
            return ctx.enter_context(nc.sbuf_tensor(name, shape, dt))

        m = Shared()
        m.xs_dram = nc.dram_tensor("xs_dram", (ROWS, P), F32, kind="Internal").ap()
        m.ys_dram = nc.dram_tensor("ys_dram", (NET * ET, P), F32, kind="Internal").ap()
        m.ident = sb("ident", [P, P])
        m.ones = sb("ones", [P, P])
        m.eps = sb("eps", [P, 1])
        m.w1 = sb("w1", [P, E0 * HID])
        m.w2 = sb("w2", [P, E0 * HID])
        m.h = sb("h", [P, TILES * P])
        m.logits = sb("logits", [P, TILES, 8])
        m.top = sb("top", [P, TILES, 8])
        m.choice = sb("choice", [P, TILES])
        m.row = sb("row", [P, TILES])
        m.slots = sb("slots", [P, TILES], U32)
        m.shift = sb("shift", [P, E0])
        m.gate = sb("gate", [P, TILES])
        m.next_row = sb("next_row", [P, E0])
        m.zeros = sb("zeros", [P, SPARE * ET // P, P])
        m.tile_e = sb("tile_e", [P, NET], I32)
        m.tile_row = sb("tile_row", [P, NET], I32)
        m.s_experts = ctx.enter_context(nc.semaphore("s_experts"))
        m.s_scattered = [ctx.enter_context(nc.semaphore(f"s_scattered{i}")) for i in (0, 1)]
        m.s_padded = ctx.enter_context(nc.semaphore("s_padded"))
        for phase in (phase1, phase2, phase3, phase4):
            with ExitStack() as ph:
                phase(nc, ctx, ph, m, t, cst, out)


def phase1(nc, ctx, ph, m, t, cst, out):
    h, logits, top, ident, eps = m.h, m.logits, m.top, m.ident, m.eps

    def sb(name, shape, dt=F32):
        return ph.enter_context(nc.sbuf_tensor(name, shape, dt))

    def psum(name, shape, dt=F32):
        return ph.enter_context(nc.psum_tensor(name, shape, dt))

    def sem(name):
        return ctx.enter_context(nc.semaphore(name))

    pe_c = sb("pe_c", [P, TPB, P])
    decay = sb("decay", [P, H, P])
    q_decay = sb("q_decay", [P, P])
    k_decay = sb("k_decay", [P, P])
    state_decay = sb("state_decay", [P, 1])
    head_mask = sb("head_mask", [P, H])
    same_head = sb("same_head", [P, P])
    center = sb("center", [P, P])
    average = sb("average", [P, P])
    w_tok = sb("w_tok", [P, GT, P])
    wq, wk, wg, wo = (sb(n, [P, P]) for n in ("wq", "wk", "wg", "wo"))
    wkv = sb("wkv", [P, 2, P])
    gn_w = sb("gn_w", [P, 1])
    gn_b = sb("gn_b", [P, 1])
    wgate = sb("wgate", [P, LP])
    gamma_b = sb("gamma_b", [P, P])
    before = sb("before", [P, P])
    before_bf = sb("before_bf", [P, P], BF16)
    ones_bf = sb("ones_bf", [P, P], BF16)
    expert_no = sb("expert_no", [P, E0])

    x_sb = [sb(f"x_sb{i}", [P, GT, F_IN]) for i in (0, 1)]
    xT_sb = sb("xT_sb", [P, P])
    stat1, stat2 = (sb(f"stat{i}", [P, GT, 6]) for i in (1, 2))
    mv1, mv2 = (sb(f"mv{i}", [P, GT, 2]) for i in (1, 2))
    lv1, lv2, lv3 = (sb(f"lv{i}", [P, GT]) for i in (1, 2, 3))
    r1, r2, r3 = (sb(f"r{i}", [P, GT]) for i in (1, 2, 3))
    nm1, nm2 = (sb(f"nm{i}", [P, GT]) for i in (1, 2))
    inv2 = sb("inv2", [P, GT])
    v3 = sb("v3", [P, GT])
    xn = sb("xn", [P, GT, P])
    xnT = [sb(f"xnT{i}", [P, GN]) for i in (0, 1)]
    qT = [sb(f"qT{i}", [P, GN]) for i in (0, 1)]
    kT = [sb(f"kT{i}", [P, GN]) for i in (0, 1)]
    gT = [sb(f"gT{i}", [P, GN]) for i in (0, 1)]
    q_in = [sb(f"q_in{i}", [P, GT, P]) for i in (0, 1)]
    q_head = [sb(f"q_head{i}", [P, H, P]) for i in (0, 1)]
    k_out = [sb(f"k_out{i}", [P, P]) for i in (0, 1)]
    v_pad = [sb(f"v_pad{i}", [P, H // 2, 4, DH]) for i in (0, 1)]
    prob = [sb(f"prob{i}", [P, H, P]) for i in (0, 1)]
    state = [sb(f"state{i}", [P, P]) for i in (0, 1)]
    s_new = sb("s_new", [P, P])
    wv_T = sb("wv_T", [P, P])
    cen = sb("cen", [P, GN])
    sq = sb("sq", [P, GN])
    lvar = sb("lvar", [P, GN])
    rstd = sb("rstd", [P, GN])
    t1 = sb("t1", [P, GN])
    t2 = sb("t2", [P, GN])
    act_T = sb("act_T", [P, GN])
    xn2 = sb("xn2", [P, GT, P])
    x2T = sb("x2T", [P, GN])
    lg = sb("lg", [P, GT, 8])
    lg_top = sb("lg_top", [P, GT, 8])
    lg_at = sb("lg_at", [P, GT, 8], U32)
    choice = sb("choice_g", [P, GT])
    onehot = sb("onehot", [P, GT + 1, E0], BF16)
    row_e = sb("row_e", [P, GT, E0])
    row_1 = sb("row_1", [P, GT, E0])
    row_f = sb("row_f", [P, GT])
    row_i = [sb(f"row_i{i}", [P, GT], U32) for i in (0, 1)]
    send = [sb(f"send{i}", [P, GT, P]) for i in (0, 1)]
    xn3 = sb("xn3", [P, GT, P])

    ps_s = [psum(f"ps_s{i}", [P, GN]) for i in (0, 1)]
    ps_j = [psum(f"ps_j{i}", [P, GN]) for i in (0, 1)]
    ps_r = psum("ps_r", [P, GN])
    ps_g = psum("ps_g", [P, GN])
    ps_m = [psum(f"ps_m{i}", [P, GN]) for i in (0, 1)]

    names = ("xt_ps xt_sb h0_ps h0 bn1 st1 ln1 r1 nm1 xn xnT_ps xnT_sb proj_ps proj_sb q_in q_head "
             "kv_ps k_out v_pad score prob pv st_ps tmp state cen var_ps lvar rstd "
             "t1 t2 silu wo_ps h1 bn2 st2 ln2 r2 nm2 inv2 xn2 x2T_ps x2T_sb v3 ln3 r3 xn3 xnn "
             "logit_ps logit top top_i kept wvT_ps wvT wv_ps wv choice onehot pos_ps row_e next_row row_1 row_f slots").split()
    S = {n: sem("p1_" + n) for n in names}

    def valid(n, k):
        return n is None or 0 <= n + k < GROUPS

    def tile(buf, u, t):
        return buf[:, bass.ds(u * GN + t * P, P)]

    x_t = t["x"].rearrange("b hh w f -> (b hh w) f").rearrange("(t p) f -> p t f", p=P)
    first_done = sem("p1_first")
    const_done = sem("p1_const")
    zero_first = sem("p1_zero_first")
    zero_done = sem("p1_zero")
    passed = sem("p1_passed")
    x_ld = [sem(f"p1_x_ld{i}") for i in (0, 1)]

    with nc.Block() as block:
        @block.sync
        def _(sp):
            consts = [(decay, cst["decay"]), (q_decay, cst["q_decay"]),
                      (k_decay, cst["k_decay"]), (state_decay, cst["state_decay"]),
                      (head_mask, cst["head_mask"]), (same_head, cst["same_head"]),
                      (center, cst["center"]), (average, cst["average"]),
                      (wq, t["L0_attn_W_Q"]), (wk, t["L0_attn_W_K"]), (wg, t["L0_attn_W_G"]),
                      (wo, t["L0_attn_W_O"]), (before, cst["before"]), (expert_no, cst["expert_no"]),
                      (m.next_row, cst["region"])]
            assert N_CONST == len(consts) + 6
            sp.dma_start(ident[:, :], cst["ident"]).then_inc(first_done, 16)
            for n in (0, 1):
                sp.dma_start(x_sb[n][:, :, :], x_t[:, GT * n:GT * n + GT, :]).then_inc(x_ld[n], 16)
            sp.wait_ge(zero_first, 1)
            for c in range(GT):
                sp.dma_start(w_tok[c * F_IN:(c + 1) * F_IN, c, :], t["L0_tok_W"]).then_inc(first_done, 16)
            sp.dma_start(pe_c[:, :, :], cst["pe"]).then_inc(first_done, 16)
            for dst, src in consts:
                dst = dst[:, :, :] if len(dst.shape) == 3 else dst[:, :]
                sp.dma_start(dst, src).then_inc(const_done, 16)
            sp.dma_start(wkv[:, 0, :], t["L0_attn_W_K"]).then_inc(const_done, 16)
            sp.dma_start(wkv[:, 1, :], t["L0_attn_W_V"]).then_inc(const_done, 16)
            sp.dma_start(gn_w[:, :], t["L0_attn_gn_weight"].unsqueeze(1)).then_inc(const_done, 16)
            sp.dma_start(gn_b[:, :], t["L0_attn_gn_bias"].unsqueeze(1)).then_inc(const_done, 16)
            sp.dma_start(gamma_b[:, :], t["L0_ffn_gamma"].partition_broadcast(P)).then_inc(const_done, 16)
            sp.wait_ge(zero_done, 1)
            sp.dma_start(wgate[:, 0:E0], t["L0_ffn_w_gating"]).then_inc(const_done, 16)
            for e in range(E0):
                sp.dma_start(m.w1[:, e * HID:(e + 1) * HID], t["L0_ffn_w1"][e]).then_inc(m.s_experts, 16)
                sp.dma_start(m.w2[:, e * HID:(e + 1) * HID].rearrange("p (k d) -> p k d", k=HB),
                             t["L0_ffn_w2"][e].rearrange("(k p) d -> p k d", p=P)).then_inc(m.s_experts, 16)
            sp.dma_start(m.xs_dram[E0 * CAP:ROWS, :].rearrange("(a p) d -> p a d", p=P),
                         m.zeros[:, :, :]).then_inc(m.s_experts, 16)

            def step(u, half, g, n):
                if n is not None and (n < 1 or n >= GROUPS - 1):
                    return
                sp.wait_ge(S["xt_ps"], u)
                sp.dma_start(x_sb[1 - g][:, :, :], x_t[:, bass.ds(GT * (u + 1), GT), :]).then_inc(x_ld[1 - g], 16)
            pipeline(sp, -1, GROUPS + 1, 2, (GROUPS - 4) // 2, step)

        @block.gpsimd
        def _(pool):
            for dst in (w_tok, xT_sb):
                pool.memset(dst[:], 0.0)
            pool.memset(eps[:, :], LN_EPS)
            pool.drain().then_inc(zero_first, 1)
            for dst in (wgate, v_pad[0], v_pad[1], m.zeros, onehot):
                pool.memset(dst[:], 0.0)
            pool.memset(ones_bf[:, :], 1.0)
            pool.memset(lg[:, :, :], NO_EXPERT)
            pool.memset(m.ones[:, :], 1.0)
            pool.drain().then_inc(zero_done, 1)
            pool.wait_ge(const_done, 16 * N_CONST)

            def scatter(u, o, c):
                if c == 0:
                    pool.wait_ge(S["slots"], u - 2)
                    pool.sem_inc(passed, 1)
                    pool.wait_ge(S["xnn"], u - 2)
                    pool.sem_inc(passed, 1)
                pool.indirect_dma_start(
                    out=m.xs_dram, out_offset=bass.IndirectOffsetOnAxis(ap=row_i[o][:, c:c + 1], axis=0),
                    in_=send[o][:, c, :], in_offset=None).then_inc(m.s_scattered[o], 16)

            def step(u, half, g, n):
                if valid(n, 0):
                    for c in range(GT):
                        if c == 0:
                            pool.wait_ge(S["proj_sb"], 3 * u + 1)
                        if above_zero(8 * u + 2 * c - 2):
                            pool.wait_ge(S["score"], 8 * u + 2 * c - 2)
                        pool.tensor_tensor(
                            q_head[c % 2][:, :, :],
                            qT[g][:, c * P:(c + 1) * P].unsqueeze(1).to_broadcast([P, H, P]),
                            head_mask[:, :].unsqueeze(2).to_broadcast([P, H, P]),
                            ALU.mult).then_inc(S["q_head"], 1)
                        if c == 0:
                            pool.tensor_tensor(
                                q_in[g][:, :, :], qT[g][:, :].rearrange("p (c t) -> p c t", c=GT),
                                q_decay[:, :].unsqueeze(1).to_broadcast([P, GT, P]),
                                ALU.mult).then_inc(S["q_in"], 1)
                        if valid(n, -3):
                            scatter(u, 1 - g, c)
                if valid(n, -3) and not valid(n, 0):
                    for c in range(GT):
                        scatter(u, 1 - g, c)
                if valid(n, -2):
                    pool.wait_ge(S["r3"], u - 1)
                    pool.tensor_tensor(xn3[:, :, :], xn2[:, :, :], r3[:, :].unsqueeze(2).to_broadcast([P, GT, P]),
                                       ALU.mult).then_inc(S["xn3"], 1)
                    pool.wait_ge(S["xn3"], u - 1)
                    if above_zero(16 * GT * (half - 1)):
                        pool.wait_ge(m.s_scattered[g], 16 * GT * (half - 1))
                    pool.tensor_tensor(send[g][:, :, :], xn3[:, :, :], gamma_b[:, :].unsqueeze(1).to_broadcast([P, GT, P]),
                                       ALU.mult).then_inc(S["xnn"], 1)
            pipeline(pool, -1, GROUPS + 2, 4, (GROUPS - 6) // 2, step)

        @block.tensor
        def _(pe):
            pe.wait_ge(first_done, 16 * N_FIRST)

            def kv(u, g, c):
                if c == 0:
                    pe.wait_ge(S["wv"], 1)
                    pe.wait_ge(S["xnT_sb"], u + 1)
                    pe.wait_ge(S["proj_sb"], 3 * u + 1)
                if above_zero(4 * u + c - 1):
                    pe.wait_ge(S["v_pad"], 4 * u + c - 1)
                if above_zero(4 * u + c - 1):
                    pe.wait_ge(S["tmp"], 4 * u + c - 1)
                pe.matmul(ps_j[c % 2][:, 0:2 * P], xnT[g][:, c * P:(c + 1) * P],
                          wkv[:, :, :], start=True, stop=True).then_inc(S["kv_ps"], 1)

            def scores(u, g, c):
                pe.wait_ge(S["q_head"], 4 * u + c + 1)
                if c == 0:
                    pe.wait_ge(S["proj_sb"], 3 * u + 2)
                for half in (0, 1):
                    if above_zero(8 * u + 2 * c + half - 1):
                        pe.wait_ge(S["prob"], 8 * u + 2 * c + half - 1)
                    pe.matmul(ps_s[half][:, :], kT[g][:, c * P:(c + 1) * P],
                              q_head[c % 2][:, 4 * half:4 * half + 4, :],
                              start=True, stop=True).then_inc(S["score"], 1)

            def state_mm(u, c, after_proj):
                pe.wait_ge(S["k_out"], 4 * u + c + 1)
                pe.wait_ge(S["v_pad"], 4 * u + c + 1)
                if above_zero(4 * u + c - 1):
                    pe.wait_ge(S["tmp"], 4 * u + c - 1)
                if after_proj:
                    pe.wait_ge(S["proj_sb"], 3 * (u + 1) + 2)
                pe.matmul(ps_j[c % 2][:, 2 * P:3 * P], k_out[c % 2][:, :],
                          v_pad[c % 2][:, :, 0:4:3, :], start=True, stop=True).then_inc(S["st_ps"], 1)

            def pv(u, g, c):
                if c == 0:
                    if above_zero(u):
                        pe.wait_ge(S["cen"], u)
                    pe.wait_ge(S["q_in"], u + 1)
                pe.wait_ge(S["prob"], 8 * u + 2 * c + 2)
                inter = not (g == 0 and c == 0)
                for r in (0, 1):
                    for pr in range(H // 2):
                        mm = pe.matmul(ps_r[32 * pr:32 * pr + 32, c * P:(c + 1) * P],
                                  v_pad[c % 2][:, pr, 2 * r:2 * r + 2, :],
                                  prob[c % 2][:, 2 * pr + r, :],
                                  start=(r == 0), stop=(r == 1 and not inter),
                                  skip_group_check=True)
                if inter:
                    pe.wait_ge(S["state"], 4 * u + c)
                    mm = pe.matmul(ps_r[:, c * P:(c + 1) * P], state[c % 2][:, :], q_in[g][:, c, :],
                                   start=False, stop=True, skip_group_check=True)
                mm.then_inc(S["pv"], 1)

            def step(u, half, g, n):
                o = 1 - g
                nxt, cur, prv, prv2 = (valid(n, k) for k in (1, 0, -1, -2))
                if cur:
                    kv(u, g, 0)
                if nxt:
                    pe.wait_ge(x_ld[o], 16 * (half + g + 1))
                    if above_zero(u - 2):
                        pe.wait_ge(S["next_row"], u - 2)
                    pe.transpose(ps_m[0][0:FX, 0:P], x_sb[o][:, :, :].rearrange("p t f -> p (t f)"),
                                 ident[:, :]).then_inc(S["xt_ps"], 1)
                if prv:
                    state_mm(u - 1, 3, cur)
                if cur:
                    scores(u, g, 0)
                if prv:
                    pv(u - 1, o, 3)
                if nxt:
                    pe.wait_ge(S["xt_sb"], u + 2)
                    if above_zero(3 * u + 3):
                        pe.wait_ge(S["proj_sb"], 3 * u + 3)
                    pe.matmul(ps_m[1][:, :], xT_sb[:, :], w_tok[:, :, :],
                              start=True, stop=True).then_inc(S["h0_ps"], 1)
                if cur:
                    kv(u, g, 1)
                    state_mm(u, 0, False)
                    scores(u, g, 1)
                if prv:
                    pe.wait_ge(S["cen"], u)
                    if above_zero(u - 1):
                        pe.wait_ge(S["h1"], u - 1)
                    pe.matmul(ps_g[:, :], average[:, :], sq[:, :], start=True, stop=True).then_inc(S["var_ps"], 1)
                if cur:
                    pv(u, g, 0)
                if cur:
                    kv(u, g, 2)
                    state_mm(u, 1, False)
                    scores(u, g, 2)
                if prv2:
                    pe.wait_ge(S["xn2"], u - 1)
                    if above_zero(u - 2):
                        pe.wait_ge(S["next_row"], u - 2)
                    if nxt:
                        pe.wait_ge(S["xt_sb"], u + 2)
                    for t in range(GT):
                        mm = pe.transpose(ps_m[0][:, t * P:(t + 1) * P], xn2[:, t, :], ident[:, :])
                    mm.then_inc(S["x2T_ps"], 1)
                if cur:
                    pv(u, g, 1)
                if cur:
                    kv(u, g, 3)
                    state_mm(u, 2, False)
                    scores(u, g, 3)
                if prv2:
                    pe.wait_ge(S["x2T_sb"], u - 1)
                    for t in range(GT):
                        mm = pe.matmul(ps_m[0][:, t * LP:(t + 1) * LP], x2T[:, t * P:(t + 1) * P],
                                       wgate[:, :], start=True, stop=True)
                    mm.then_inc(S["logit_ps"], 1)
                if nxt:
                    pe.wait_ge(S["xn"], u + 2)
                    for t in range(GT):
                        mm = pe.transpose(ps_m[1][:, t * P:(t + 1) * P], xn[:, t, :], ident[:, :])
                    mm.then_inc(S["xnT_ps"], 1)
                if cur:
                    pv(u, g, 2)
                if prv:
                    pe.wait_ge(S["silu"], u)
                    for t in range(GT):
                        mm = pe.matmul(ps_g[:, t * P:(t + 1) * P], act_T[:, t * P:(t + 1) * P], wo[:, :],
                                       start=True, stop=True)
                    mm.then_inc(S["wo_ps"], 1)
                if n == -1:
                    pe.wait_ge(const_done, 16 * N_CONST)
                    pe.transpose(ps_g[:, 0:P], wkv[:, 1, :], ident[:, :]).then_inc(S["wvT_ps"], 1)
                    pe.wait_ge(S["wvT"], 1)
                    pe.matmul(ps_g[:, P:2 * P], wv_T[:, :], center[:, :], start=True,
                              stop=True).then_inc(S["wv_ps"], 1)
                if nxt:
                    pe.wait_ge(S["xnT_sb"], u + 2)
                    if above_zero(4 * u + 3):
                        pe.wait_ge(S["tmp"], 4 * u + 3)
                    pe.matmul(ps_j[0][:, :], wq[:, :], xnT[o][:, :], start=True, stop=True).then_inc(S["proj_ps"], 1)
                    if above_zero(4 * u + 4):
                        pe.wait_ge(S["k_out"], 4 * u + 4)
                    if above_zero(4 * u + 4):
                        pe.wait_ge(S["v_pad"], 4 * u + 4)
                    pe.matmul(ps_j[1][:, :], wk[:, :], xnT[o][:, :], start=True, stop=True).then_inc(S["proj_ps"], 1)
                    pe.matmul(ps_m[1][:, :], wg[:, :], xnT[o][:, :], start=True, stop=True).then_inc(S["proj_ps"], 1)
                if prv2:
                    pe.wait_ge(S["onehot"], u - 1)
                    pe.matmul(ps_m[0][:, POS0:POS0 + (GT + 1) * E0], before_bf[:, :], onehot[:, :, :],
                              start=True, stop=False, skip_group_check=True)
                    for t in range(GT):
                        mm = pe.matmul(ps_m[0][:, POS0 + (t + 1) * E0:POS0 + (GT + 1) * E0], ones_bf[:, :],
                                       onehot[:, t:t + 1, :].to_broadcast([P, GT - t, E0]),
                                       start=False, stop=(t == GT - 1), skip_group_check=True)
                    mm.then_inc(S["pos_ps"], 1)
            pipeline(pe, -1, GROUPS + 1, 2, (GROUPS - 4) // 2, step)

        @block.scalar
        def _(act):
            act.preload_act_table_set(LN_EXP)
            act.wait_ge(zero_first, 1)

            def copy(dst, src, s):
                act.activation(dst, src, ACT.Copy).then_inc(S[s], 1)

            def rsqrt(var, ln, out_, s_stat, s_ln, s_out, count):
                act.wait_ge(S[s_stat], count)
                act.activation(ln[:, :], var, ACT.Ln, bias=eps[:, 0:1]).then_inc(S[s_ln], 1)
                act.wait_ge(S[s_ln], count)
                act.activation(out_[:, :], ln[:, :], ACT.Exp, scale=-0.5).then_inc(S[s_out], 1)

            def normal(dst, src, r, nm, s_nm, s_out, count):
                act.wait_ge(S[s_nm], count)
                for t in range(GT):
                    ins = act.activation(dst(t), src(t), ACT.Identity, scale=r[:, t:t + 1], bias=nm[:, t:t + 1])
                ins.then_inc(S[s_out], 1)

            def vpad(u, c):
                act.wait_ge(S["k_out"], 4 * u + c + 1)
                if above_zero(4 * u + c - 1):
                    act.wait_ge(S["pv"], 4 * u + c - 1)
                copy(v_pad[c % 2][:, :, 0:4:3, :],
                     ps_j[c % 2][:, P:2 * P].rearrange("p (a r x) -> p a r x", a=H // 2, r=2), "v_pad")

            def step(u, half, g, n):
                o = 1 - g
                nxt, cur, prv, prv2 = (valid(n, k) for k in (1, 0, -1, -2))
                if nxt:
                    act.wait_ge(S["xt_ps"], u + 2)
                    if above_zero(u + 1):
                        act.wait_ge(S["h0_ps"], u + 1)
                    copy(xT_sb[0:FX, :], ps_m[0][0:FX, 0:P], "xt_sb")
                if cur:
                    vpad(u, 0)
                if prv2:
                    rsqrt(mv2[:, :, 1], lv2, r2, "st2", "ln2", "r2", u - 1)
                    act.activation(inv2[:, :], lv2[:, :], ACT.Exp, scale=-1.0).then_inc(S["inv2"], 1)
                if prv:
                    act.wait_ge(S["pv"], 4 * u)
                    if above_zero(u - 1):
                        act.wait_ge(S["var_ps"], u - 1)
                    if above_zero(u - 1):
                        act.wait_ge(S["t1"], u - 1)
                    act.activation(sq[:, :], ps_r[:, :], ACT.Square)
                    copy(cen[:, :], ps_r[:, :], "cen")
                if cur:
                    vpad(u, 1)
                if prv2:
                    if above_zero(u - 2):
                        act.wait_ge(S["x2T_ps"], u - 2)
                    if above_zero(u - 2):
                        act.wait_ge(S["xnn"], u - 2)
                    normal(lambda t: xn2[:, t, :], lambda t: tile(h, u - 2, t), r2, nm2, "nm2", "xn2", u - 1)
                if prv:
                    act.wait_ge(S["var_ps"], u)
                    act.activation(lvar[:, :], ps_g[:, :], ACT.Ln, bias=eps[:, 0:1]).then_inc(S["lvar"], 1)
                    act.wait_ge(S["lvar"], u)
                    act.activation(rstd[:, :], lvar[:, :], ACT.Exp, scale=-0.5).then_inc(S["rstd"], 1)
                if cur:
                    vpad(u, 2)
                if nxt:
                    rsqrt(mv1[:, :, 1], lv1, r1, "st1", "ln1", "r1", u + 2)
                if prv2:
                    act.wait_ge(S["x2T_ps"], u - 1)
                    copy(x2T[:, :], ps_m[0][:, :], "x2T_sb")
                    rsqrt(v3[:, :], lv3, r3, "v3", "ln3", "r3", u - 1)
                if prv:
                    act.preload_act_table_set("silu_and_others")
                if nxt:
                    if above_zero(u + 1):
                        act.wait_ge(S["xnT_ps"], u + 1)
                    normal(lambda t: xn[:, t, :], lambda t: tile(h, u + 1, t), r1, nm1, "nm1", "xn", u + 2)
                if prv:
                    act.wait_ge(S["t2"], u)
                    if above_zero(u - 1):
                        act.wait_ge(S["wo_ps"], u - 1)
                    act.activation(act_T[:, :], t2[:, :], ACT.Silu).then_inc(S["silu"], 1)
                if n == -1:
                    act.wait_ge(S["wvT_ps"], 1)
                    copy(wv_T[:, :], ps_g[:, 0:P], "wvT")
                    act.wait_ge(S["wv_ps"], 1)
                    copy(wkv[:, 1, :], ps_g[:, P:2 * P], "wv")
                    act.wait_ge(zero_done, 1)
                if cur:
                    vpad(u, 3)
                if nxt:
                    act.wait_ge(S["xnT_ps"], u + 2)
                    copy(xnT[o][:, :], ps_m[1][:, :], "xnT_sb")
                    for i, (dst, bank) in enumerate(((qT, ps_j[0]), (kT, ps_j[1]), (gT, ps_m[1]))):
                        act.wait_ge(S["proj_ps"], 3 * u + 4 + i)
                        if i == 0:
                            if above_zero(4 * u):
                                act.wait_ge(S["q_head"], 4 * u)
                            if above_zero(u):
                                act.wait_ge(S["q_in"], u)
                        copy(dst[o][:, :], bank[:, :], "proj_sb")
                if prv:
                    act.preload_act_table_set(LN_EXP)
            pipeline(act, -1, GROUPS + 1, 2, (GROUPS - 4) // 2, step)

        @block.vector
        def _(dve):
            dve.wait_ge(first_done, 16 * N_FIRST)

            def stats(src, stat, mv, s_src, s_bn, s_out, count):
                dve.wait_ge(S[s_src], count)
                dve.sem_inc(passed, 1)
                for t in range(GT):
                    ins = dve.bn_stats(stat[:, t, :], src(t))
                ins.then_inc(S[s_bn], 1)
                dve.wait_ge(S[s_bn], count)
                dve.sem_inc(passed, 1)
                for t in range(GT):
                    ins = dve.bn_aggr(mv[:, t, :], stat[:, t, :])
                ins.then_inc(S[s_out], 1)

            def shift(nm, mv, r, s_r, s_out, count):
                dve.wait_ge(S[s_r], count)
                dve.scalar_tensor_tensor(nm[:, :], mv[:, :, 0], -1.0, r[:, :], ALU.mult,
                                         ALU.mult).then_inc(S[s_out], 1)

            def new_state(u, c):
                dve.wait_ge(S["st_ps"], 4 * u + c + 1)
                if above_zero(4 * u + c):
                    dve.wait_ge(S["state"], 4 * u + c)
                dve.tensor_tensor(s_new[:, :], ps_j[c % 2][:, 2 * P:3 * P], same_head[:, :],
                                  ALU.mult).then_inc(S["tmp"], 1)

            def chunk(u, g, c):
                dve.wait_ge(S["kv_ps"], 4 * u + c + 1)
                if above_zero(4 * u + c - 1):
                    dve.wait_ge(S["st_ps"], 4 * u + c - 1)
                dve.tensor_tensor(k_out[c % 2][:, :], ps_j[c % 2][:, 0:P], k_decay[:, :],
                                  ALU.mult).then_inc(S["k_out"], 1)
                if c > 0:
                    new_state(u, c - 1)
                if above_zero(4 * u + c - 1):
                    dve.wait_ge(S["pv"], 4 * u + c - 1)
                for half in (0, 1):
                    dve.wait_ge(S["score"], 8 * u + 2 * c + half + 1)
                    dve.tensor_tensor(prob[c % 2][:, 4 * half:4 * half + 4, :],
                                      ps_s[half][:, :].rearrange("p (a t) -> p a t", a=4),
                                      decay[:, 4 * half:4 * half + 4, :], ALU.mult).then_inc(S["prob"], 1)

            def state_up(u, g, c):
                if above_zero(4 * u + c):
                    dve.wait_ge(S["pv"], 4 * u + c)
                dve.wait_ge(S["tmp"], 4 * u + c + 1)
                if above_zero(4 * u + c):
                    dve.wait_ge(S["state"], 4 * u + c)
                dst = state[(c + 1) % 2]
                if g == 0 and c == 0:
                    dve.tensor_copy(dst[:, :], s_new[:, :]).then_inc(S["state"], 1)
                else:
                    dve.scalar_tensor_tensor(dst[:, :], state[c % 2][:, :], state_decay[:, 0:1], s_new[:, :],
                                             ALU.mult, ALU.add).then_inc(S["state"], 1)

            def step(u, half, g, n):
                o = 1 - g
                nxt, cur, prv, prv2 = (valid(n, k) for k in (1, 0, -1, -2))
                if n == 0:
                    dve.wait_ge(const_done, 16 * N_CONST)
                    dve.wait_ge(zero_done, 1)
                    dve.tensor_copy(before_bf[:, :], before[:, :])
                if prv2:
                    stats(lambda t: tile(h, u - 2, t), stat2, mv2, "h1", "bn2", "st2", u - 1)
                if cur:
                    chunk(u, g, 0)
                if prv:
                    new_state(u - 1, 3)
                    state_up(u - 1, o, 3)
                if cur:
                    chunk(u, g, 1)
                if prv2:
                    shift(nm2, mv2, r2, "r2", "nm2", u - 1)
                    dve.wait_ge(S["inv2"], u - 1)
                    dve.tensor_tensor(v3[:, :], mv2[:, :, 1], inv2[:, :], ALU.mult).then_inc(S["v3"], 1)
                if cur:
                    state_up(u, g, 0)
                if nxt:
                    dve.wait_ge(S["h0_ps"], u + 2)
                    dve.tensor_tensor(h[:, bass.ds((u + 1) * GN, GN)], ps_m[1][:, :],
                                      pe_c[:, o * GT:(o + 1) * GT, :].rearrange("p t d -> p (t d)"),
                                      ALU.add).then_inc(S["h0"], 1)
                    stats(lambda t: tile(h, u + 1, t), stat1, mv1, "h0", "bn1", "st1", u + 2)
                if cur:
                    chunk(u, g, 2)
                    state_up(u, g, 1)
                if nxt:
                    shift(nm1, mv1, r1, "r1", "nm1", u + 2)
                if prv:
                    dve.wait_ge(S["rstd"], u)
                    dve.scalar_tensor_tensor(t1[:, :], cen[:, :], gn_w[:, 0:1], rstd[:, :],
                                             ALU.mult, ALU.mult).then_inc(S["t1"], 1)
                    dve.wait_ge(S["t1"], u)
                    dve.scalar_tensor_tensor(t2[:, :], t1[:, :], gn_b[:, 0:1], gT[o][:, :],
                                             ALU.add, ALU.add).then_inc(S["t2"], 1)
                if cur:
                    chunk(u, g, 3)
                    state_up(u, g, 2)
                if prv2:
                    dve.wait_ge(S["logit_ps"], u - 1)
                    if above_zero(u - 2):
                        dve.wait_ge(S["kept"], u - 2)
                    dve.tensor_copy(lg[:, :, 0:E0],
                                    ps_m[0][:, 0:GT * LP].rearrange("p (t e) -> p t e", t=GT)[:, :, 0:E0]
                                    ).then_inc(S["logit"], 1)
                    dve.wait_ge(S["logit"], u - 1)
                    dve.sem_inc(passed, 1)
                    for tt in range(GT):
                        ins = dve.max(lg_top[:, tt, :], lg[:, tt, :])
                    ins.then_inc(S["top"], 1)
                    dve.wait_ge(S["top"], u - 1)
                    dve.sem_inc(passed, 1)
                    for tt in range(GT):
                        ins = dve.max_index(lg_at[:, tt, :], lg_top[:, tt, :], lg[:, tt, :])
                    ins.then_inc(S["top_i"], 1)
                    tiles = bass.ds((u - 2) * GT, GT)
                    dve.tensor_copy(logits[:, tiles, :], lg[:, :, :])
                    dve.tensor_copy(top[:, tiles, :], lg_top[:, :, :]).then_inc(S["kept"], 1)
                    dve.wait_ge(S["top_i"], u - 1)
                    dve.tensor_copy(choice[:, :], lg_at[:, :, 0]).then_inc(S["choice"], 1)
                    dve.wait_ge(S["choice"], u - 1)
                    dve.tensor_copy(m.choice[:, tiles], choice[:, :])
                    if above_zero(u - 2):
                        dve.wait_ge(S["pos_ps"], u - 2)
                    dve.tensor_tensor(onehot[:, 0:GT, :], choice[:, :].unsqueeze(2).to_broadcast([P, GT, E0]),
                                      expert_no[:, :].unsqueeze(1).to_broadcast([P, GT, E0]),
                                      ALU.is_equal).then_inc(S["onehot"], 1)
                if prv:
                    dve.wait_ge(S["wo_ps"], u)
                    hg = h[:, bass.ds((u - 1) * GN, GN)]
                    dve.tensor_tensor(hg, ps_g[:, :], hg, ALU.add).then_inc(S["h1"], 1)
                if prv2:
                    def before_it(first, last):
                        return ps_m[0][:, POS0 + first * E0:POS0 + last * E0]
                    dve.wait_ge(S["pos_ps"], u - 1)
                    if above_zero(u - 2):
                        dve.wait_ge(S["next_row"], u - 2)
                    dve.tensor_tensor(row_e[:, :, :], before_it(0, GT).rearrange("p (t e) -> p t e", t=GT),
                                      m.next_row[:, :].unsqueeze(1).to_broadcast([P, GT, E0]),
                                      ALU.add).then_inc(S["row_e"], 1)
                    dve.wait_ge(S["row_e"], u - 1)
                    dve.tensor_tensor(m.next_row[:, :], before_it(GT, GT + 1), m.next_row[:, :],
                                      ALU.add).then_inc(S["next_row"], 1)
                    dve.tensor_tensor(row_1[:, :, :], row_e[:, :, :], onehot[:, 0:GT, :],
                                      ALU.mult).then_inc(S["row_1"], 1)
                    dve.wait_ge(S["row_1"], u - 1)
                    dve.tensor_reduce(row_f[:, :], row_1[:, :, :], AXX, ALU.add).then_inc(S["row_f"], 1)
                    dve.wait_ge(S["row_f"], u - 1)
                    dve.tensor_copy(m.row[:, bass.ds((u - 2) * GT, GT)], row_f[:, :])
                    if above_zero(16 * GT * (half - 1)):
                        dve.wait_ge(m.s_scattered[g], 16 * GT * (half - 1))
                    dve.tensor_copy(row_i[g][:, :], row_f[:, :]).then_inc(S["slots"], 1)
            pipeline(dve, -1, GROUPS + 1, 2, (GROUPS - 4) // 2, step)


def phase2(nc, ctx, ph, m, t, cst, out):
    def sb(name, shape, dt=F32):
        return ph.enter_context(nc.sbuf_tensor(name, shape, dt))

    def sem(name):
        return ctx.enter_context(nc.semaphore(name))

    tile_no = sb("tile_no", [P, NET])
    region = sb("region", [P, E0])
    end_i = sb("end_i", [P, E0], I32)
    n_f = sb("n_f", [P, E0])
    n_i = sb("n_i", [P, E0], I32)
    n_tiles_i = sb("n_tiles_i", [P, E0], I32)
    n_tiles = sb("n_tiles", [P, E0])
    ends = sb("ends", [P, E0])
    starts = sb("starts", [P, E0])
    skip = sb("skip", [P, E0])
    past = sb("past", [P, NET, E0])
    skips = sb("skips", [P, NET, E0])
    tile_f = sb("tile_f", [P, NET])
    tile_off = sb("tile_off", [P, NET])
    row_s = sb("row_s", [P, NET])
    row_f = sb("row_f2", [P, NET])
    diff = sb("diff", [P, TILES, E0])
    expd = sb("expd", [P, TILES, E0])
    total = sb("total", [P, TILES])
    d2 = sb("d2", [P, TILES])
    e2 = sb("e2", [P, TILES])
    den = sb("den", [P, TILES])
    loaded, ended, differences, exps, steps = (
        sem("p2_" + n) for n in ("loaded", "ended", "differences", "exps", "steps"))

    with nc.Block() as block:
        @block.sync
        def _(sp):
            sp.dma_start(tile_no[:, :], cst["tile_no"]).then_inc(loaded, 16)
            sp.dma_start(region[:, :], cst["region"]).then_inc(loaded, 16)
            sp.wait_ge(ended, 1)
            for e in range(E0):
                end = sp.value_load(end_i[0:1, e:e + 1], min_val=e * CAP, max_val=e * CAP + TILES * P)
                sp.dma_start(m.xs_dram[bass.ds(end, ET), :].rearrange("(a p) d -> p a d", p=P),
                             m.zeros[:, 0:ET // P, :]).then_inc(m.s_padded, 16)

        @block.scalar
        def _(act):
            act.wait_ge(differences, 1)
            act.activation(expd[:, :, :], diff[:, :, :], ACT.Exp).then_inc(exps, 1)
            act.activation(e2[:, :], d2[:, :], ACT.Exp).then_inc(exps, 1)

        @block.vector
        def _(dve):
            done = [0]

            def then(ins):
                done[0] += 1
                ins.then_inc(steps, 1)
                dve.wait_ge(steps, done[0])

            dve.tensor_copy(end_i[:, :], m.next_row[:, :]).then_inc(ended, 1)
            dve.wait_ge(loaded, 32)
            then(dve.tensor_tensor(n_f[:, :], m.next_row[:, :], region[:, :], ALU.subtract))
            then(dve.tensor_scalar(n_i[:, :], n_f[:, :], float(ET - 1), None, ALU.add))
            then(dve.tensor_scalar(n_tiles_i[:, :], n_i[:, :], ET.bit_length() - 1, None, ALU.logical_shift_right))
            then(dve.tensor_copy(n_tiles[:, :], n_tiles_i[:, :]))
            then(dve.tensor_tensor_scan(ends[:, :], m.ones[:, 0:E0], n_tiles[:, :], 0.0, ALU.mult, ALU.add))
            then(dve.tensor_tensor(starts[:, :], ends[:, :], n_tiles[:, :], ALU.subtract))
            dve.scalar_tensor_tensor(m.shift[:, :], starts[:, :], float(ET), region[:, :], ALU.mult, ALU.subtract)
            dve.tensor_scalar(skip[:, :], n_tiles[:, :], -float(ET), float(CAP), ALU.mult, ALU.add)
            then(dve.tensor_tensor(past[:, :, :], tile_no[:, :].unsqueeze(2).to_broadcast([P, NET, E0]),
                                   ends[:, :].unsqueeze(1).to_broadcast([P, NET, E0]), ALU.is_ge))
            dve.tensor_tensor(skips[:, :, :], past[:, :, :], skip[:, :].unsqueeze(1).to_broadcast([P, NET, E0]),
                              ALU.mult)
            then(dve.tensor_reduce(tile_f[:, :], past[:, :, 0:E0 - 1], AXX, ALU.add))
            dve.tensor_scalar(tile_off[:, :], tile_f[:, :], float(HID), None, ALU.mult)
            then(dve.tensor_reduce(row_s[:, :], skips[:, :, :], AXX, ALU.add))
            dve.tensor_copy(m.tile_e[:, :], tile_off[:, :])
            then(dve.scalar_tensor_tensor(row_f[:, :], tile_no[:, :], float(ET), row_s[:, :], ALU.mult, ALU.add))
            dve.tensor_copy(m.tile_row[:, :], row_f[:, :])
            dve.tensor_tensor(d2[:, :], m.top[:, :, 1], m.top[:, :, 0], ALU.subtract)
            dve.tensor_tensor(diff[:, :, :], m.logits[:, :, 0:E0],
                              m.top[:, :, 0:1].to_broadcast([P, TILES, E0]), ALU.subtract).then_inc(differences, 1)
            dve.wait_ge(exps, 2)
            then(dve.tensor_reduce(total[:, :], expd[:, :, :], AXX, ALU.add))
            then(dve.scalar_tensor_tensor(den[:, :], total[:, :], GATE_EPS, e2[:, :], ALU.mult, ALU.add))
            then(dve.tensor_scalar(den[:, :], den[:, :], 1.0, None, ALU.add))
            then(dve.reciprocal(m.gate[:, :], den[:, :]))


def phase3(nc, ctx, ph, m, t, cst, out):
    def sb(name, shape, dt=F32):
        return ph.enter_context(nc.sbuf_tensor(name, shape, dt))

    def psum(name, shape, dt=F32):
        return ph.enter_context(nc.psum_tensor(name, shape, dt))

    def sem(name):
        return ctx.enter_context(nc.semaphore(name))

    RS = ET // P
    xe = [sb(f"xe{i}", [P, RS, P]) for i in (0, 1)]
    xeT = [sb(f"xeT{i}", [P, ET]) for i in (0, 1)]
    w1c = [sb(f"w1c{i}", [P, HID]) for i in (0, 1)]
    hid = [sb(f"hid{i}", [P, HB, ET]) for i in (0, 1)]
    y_sb = [sb(f"y_sb{i}", [P, RS, P]) for i in (0, 1)]
    ps_t = [psum(f"ps_t{i}", [P, 512]) for i in (0, 1)]
    ps_h = [psum(f"ps_h{i}", [P, HB, ET]) for i in (0, 1)]
    ps_y = [psum(f"ps_y{i}", [P, 512]) for i in (0, 1)]
    passed = sem("p3_passed")
    xe_ld = [sem(f"p3_xe_ld{i}") for i in (0, 1)]
    y_st = [sem(f"p3_y_st{i}") for i in (0, 1)]
    names = "xT_ps xT_sb w1c h_ps hid y_ps y_sb shift_e slot_f".split()
    S = {n: sem("p3_" + n) for n in names}
    ys_t = m.ys_dram.rearrange("(a p) d -> p a d", p=P)
    shift_e = sb("shift_e", [P, TILES])
    PAIRS = (NET - 4) // 2

    def valid(n, k):
        return n is None or 0 <= n + k < NET

    def offset(eng, j):
        return eng.value_load(m.tile_e[0:1, bass.ds(j, 1)], min_val=0, max_val=(E0 - 1) * HID)

    with nc.Block() as block:
        @block.gpsimd
        def _(pool):
            for e in range(E0):
                if e > 0:
                    pool.wait_ge(S["slot_f"], e)
                pool.tensor_scalar(shift_e[:, :], m.choice[:, :], float(e), m.shift[:, e:e + 1],
                                   ALU.is_equal, ALU.mult).then_inc(S["shift_e"], 1)
                pool.wait_ge(S["shift_e"], e + 1)
                pool.tensor_tensor(m.row[:, :], m.row[:, :], shift_e[:, :], ALU.add).then_inc(S["slot_f"], 1)
            pool.wait_ge(S["slot_f"], E0)
            pool.tensor_copy(m.slots[:, :], m.row[:, :])

        @block.sync
        def _(sp):
            for i in (0, 1):
                sp.wait_ge(m.s_scattered[i], 16 * TILES // 2)
            sp.wait_ge(m.s_padded, 16 * E0)
            sp.wait_ge(m.s_experts, 16 * N_EXPERT)

            def rows(j):
                row = sp.value_load(m.tile_row[0:1, bass.ds(j, 1)], min_val=0, max_val=ROWS - ET)
                return m.xs_dram[bass.ds(row, ET), :].rearrange("(a p) d -> p a d", p=P)

            for n in (0, 1):
                sp.dma_start(xe[n][:, :, :], rows(n)).then_inc(xe_ld[n], 16)

            def step(j, half, g, n):
                if valid(n, 0) and valid(n, 2):
                    src = rows(j + 2)
                    sp.wait_ge(S["xT_ps"], j + 1)
                    sp.dma_start(xe[g][:, :, :], src).then_inc(xe_ld[g], 16)
                if valid(n, -2):
                    sp.wait_ge(S["y_sb"], j - 1)
                    sp.dma_start(ys_t[:, bass.ds(RS * (j - 2), RS), :], y_sb[g][:, :, :]).then_inc(y_st[g], 16)
            pipeline(sp, -1, NET + 1, 2, PAIRS, step)
            for i in (0, 1):
                sp.wait_ge(y_st[i], 16 * (NET // 2))

        @block.tensor
        def _(pe):
            def step(j, half, g, n):
                o = 1 - g
                if valid(n, -1):
                    off = offset(pe, j - 1)
                if valid(n, 1):
                    pe.wait_ge(xe_ld[o], 16 * (half + g + 1))
                    if above_zero(j):
                        pe.wait_ge(S["xT_sb"], j)
                    for s in range(RS):
                        mm = pe.transpose(ps_t[o][:, s * P:(s + 1) * P], xe[o][:, s, :], m.ident[:, :])
                    mm.then_inc(S["xT_ps"], 1)
                if valid(n, 0):
                    pe.wait_ge(S["xT_sb"], j + 1)
                    pe.wait_ge(S["w1c"], j + 1)
                    if above_zero(j - 1):
                        pe.wait_ge(S["hid"], j - 1)
                    for k in range(HB):
                        mm = pe.matmul(ps_h[g][:, k, :], w1c[g][:, k * P:(k + 1) * P], xeT[g][:, :],
                                       start=True, stop=True)
                    mm.then_inc(S["h_ps"], 1)
                if valid(n, -1):
                    pe.wait_ge(S["hid"], j)
                    if above_zero(j - 2):
                        pe.wait_ge(S["y_sb"], j - 2)
                    for s in range(RS):
                        for k in range(HB):
                            mm = pe.matmul(ps_y[o][:, s * P:(s + 1) * P], hid[o][:, k, s * P:(s + 1) * P],
                                           m.w2[:, bass.ds(off + k * P, P)], start=(k == 0), stop=(k == HB - 1))
                    mm.then_inc(S["y_ps"], 1)
            pipeline(pe, -1, NET, 2, PAIRS, step)

        @block.scalar
        def _(act):
            act.preload_act_table_set("gelu_and_others")

            def step(j, half, g, n):
                o = 1 - g
                if valid(n, 1):
                    act.wait_ge(S["xT_ps"], j + 2)
                    if above_zero(j):
                        act.wait_ge(S["h_ps"], j)
                    act.activation(xeT[o][:, :], ps_t[o][:, 0:ET], ACT.Copy).then_inc(S["xT_sb"], 1)
                if valid(n, 0):
                    act.wait_ge(S["h_ps"], j + 1)
                    if above_zero(j - 1):
                        act.wait_ge(S["y_ps"], j - 1)
                    act.activation(hid[g][:, :, :], ps_h[g][:, :, :], ACT.Gelu).then_inc(S["hid"], 1)
            pipeline(act, -1, NET, 2, PAIRS, step)

        @block.vector
        def _(dve):
            def step(j, half, g, n):
                o = 1 - g
                if valid(n, 1):
                    if above_zero(j):
                        dve.wait_ge(S["h_ps"], j)
                    off = offset(dve, j + 1)
                    dve.tensor_copy(w1c[o][:, :], m.w1[:, bass.ds(off, HID)]).then_inc(S["w1c"], 1)
                if valid(n, -1):
                    dve.wait_ge(S["y_ps"], j)
                    if above_zero(16 * (half + g - 1)):
                        dve.wait_ge(y_st[o], 16 * (half + g - 1))
                    dve.tensor_copy(y_sb[o][:, :, :], ps_y[o][:, 0:ET].rearrange("p (s d) -> p s d", s=RS)
                                    ).then_inc(S["y_sb"], 1)
            dve.wait_ge(m.s_experts, 16 * N_EXPERT)
            pipeline(dve, -1, NET, 2, PAIRS, step)


def phase4(nc, ctx, ph, m, t, cst, out):
    h, ident, ones, eps = m.h, m.ident, m.ones, m.eps
    back = ph.enter_context(nc.sbuf_tensor("back", [P, TILES * P], F32))

    def sb(name, shape, dt=F32):
        return ph.enter_context(nc.sbuf_tensor("p4_" + name, shape, dt))

    def psum(name, shape, dt=F32):
        return ph.enter_context(nc.psum_tensor("p4_" + name, shape, dt))

    def sem(name):
        return ctx.enter_context(nc.semaphore(name))

    w_ld = sb("w_ld", [P, 3, P])
    w_T = sb("w_T", [P, 3, P])
    b_q = sb("b_q", [P, 1])
    b_k = sb("b_k", [P, 1])
    b_v = sb("b_v", [P, P])
    w_r = sb("w_r", [P, LP])
    b_r = sb("b_r", [P, E1])
    stat = sb("stat", [P, TPB, 6])
    mv = sb("mv", [P, TPB, 2])
    lv = sb("lv", [P, TPB])
    rs = sb("rs", [P, TPB])
    nm = sb("nm", [P, TPB])
    stat_f = sb("stat_f", [P, TPB, 6])
    mv_f = sb("mv_f", [P, TPB, 2])
    lv_f = sb("lv_f", [P, TPB])
    rs_f = sb("rs_f", [P, TPB])
    nm_f = sb("nm_f", [P, TPB])
    xf = sb("xf", [P, TPB, P])
    xn = sb("xn", [P, TPB, P])
    xnT = sb("xnT", [P, SEQ])
    qT = [sb(f"qT{i}", [P, SEQ]) for i in (0, 1)]
    kT = [sb(f"kT{i}", [P, SEQ]) for i in (0, 1)]
    val = [sb(f"val{i}", [P, TPB, P]) for i in (0, 1)]
    top_s = sb("top_s", [P, TPB])
    bias_s = sb("bias_s", [P, TPB])
    sum_s = sb("sum_s", [P, TPB])
    inv_s = sb("inv_s", [P, TPB])
    prob = [sb(f"prob{i}", [P, SEQ]) for i in (0, 1)]
    val_n = [sb(f"val_n{i}", [P, P]) for i in (0, 1)]
    h3c = sb("h3c", [P, TPB, P])
    xfT = sb("xfT", [P, SEQ])
    xf_sum = sb("xf_sum", [P, 2])
    mean1 = sb("mean1", [P, 1])
    mean = sb("mean", [P, P])
    lg = sb("lg", [P, E1])
    lg_top = sb("lg_top", [P, 1])
    ex = sb("ex", [P, E1])
    ex_sum = sb("ex_sum", [P, 1])
    ex_top = sb("ex_top", [P, 8])
    ex_at = sb("ex_at", [P, 8], U32)
    gate = [sb(f"gate{i}", [P, 1]) for i in (0, 1)]
    we = [sb(f"we{i}", [P, P]) for i in (0, 1)]
    be = [sb(f"be{i}", [P, P]) for i in (0, 1)]
    y1 = sb("y1", [P, SEQ])
    o_sb = [sb(f"o_sb{i}", [P, TPB, P]) for i in (0, 1)]

    ps_s = [psum(f"ps_s{i}", [P, SEQ]) for i in (0, 1)]
    ps_o = psum("ps_o", [P, SEQ])
    ps_f = [psum(f"ps_f{i}", [P, 512]) for i in (0, 1)]

    const_done, zero_done, passed = sem("p4_const_ld"), sem("p4_zeroed"), sem("p4_passed")
    gathered = [sem(f"p4_gathered{i}") for i in (0, 1)]
    we_ld = [sem(f"p4_we_ld{i}") for i in (0, 1)]
    o_st = [sem(f"p4_o_st{i}") for i in (0, 1)]
    names = ("wT_ps wT_sb h2 bn st ln rs nm xn xT_ps xT_sb q_ps q_sb k_ps k_sb v_ps v_sb score top "
             "bias exp inv val_n av h3 bn_f st_f ln_f rs_f nm_f xf hT_ps hT_sb mean1 mean r_ps lg lg_top ex ex_top ex_at gate "
             "y_ps y1 out").split()
    S = {n: sem("p4_did_" + n) for n in names}
    N_C4 = 9
    out_t = out.rearrange("b (c p) d -> b p c d", p=P)
    PAIRS = (B - 4) // 2

    def valid(n, k):
        return n is None or 0 <= n + k < B

    def tile(buf, u, tt):
        return buf[:, bass.ds(u * SEQ + tt * P, P)]

    with nc.Block() as block:
        @block.sync
        def _(sp):
            sp.dma_start(w_ld[:, 0, :], t["L1_attn_Wq"]).then_inc(const_done, 16)
            sp.dma_start(w_ld[:, 1, :], t["L1_attn_Wk"]).then_inc(const_done, 16)
            sp.dma_start(w_ld[:, 2, :], t["L1_attn_Wv"]).then_inc(const_done, 16)
            sp.dma_start(b_q[:, :], t["L1_attn_bq"].unsqueeze(1)).then_inc(const_done, 16)
            sp.dma_start(b_k[:, :], t["L1_attn_bk"].unsqueeze(1)).then_inc(const_done, 16)
            sp.dma_start(b_v[:, :], t["L1_attn_bv"].partition_broadcast(P)).then_inc(const_done, 16)
            sp.dma_start(b_r[:, :], t["L1_ffn_bg"].partition_broadcast(P)).then_inc(const_done, 16)
            sp.wait_ge(zero_done, 1)
            sp.dma_start(w_r[:, 0:E1], t["L1_ffn_Wg"]).then_inc(const_done, 16)

            def step(u, half, g, n):
                o = 1 - g
                if valid(n, -1):
                    if above_zero(u - 2):
                        sp.wait_ge(S["out"], u - 2)
                    sp.sem_inc(passed, 1)
                    sp.wait_ge(S["ex_at"], u)
                    sp.sem_inc(passed, 1)
                    at = sp.value_load(ex_at[0:1, 0:1], min_val=0, max_val=E1 - 1)
                    sp.dma_start(we[o][:, :], t["L1_ffn_We"][bass.ds(at, 1), :, :].rearrange("a d o -> (a d) o")
                                 ).then_inc(we_ld[o], 16)
                    sp.dma_start(be[o][:, :], t["L1_ffn_be"][bass.ds(at, 1), :].rearrange("a o -> (a o)")
                                 .partition_broadcast(P)).then_inc(we_ld[o], 16)
                    sp.wait_ge(S["out"], u)
                    sp.dma_start(out_t[bass.ds(u - 1, 1), :, :, :].rearrange("b p c d -> (b p) c d"),
                                 o_sb[o][:, :, :]).then_inc(o_st[o], 16)
            pipeline(sp, -1, B, 2, PAIRS, step)
            for i in (0, 1):
                sp.wait_ge(o_st[i], 16 * (B // 2))

        @block.gpsimd
        def _(pool):
            pool.memset(w_r[:, :], 0.0).then_inc(zero_done, 1)
            for u in range(B):
                if u >= 2:
                    pool.wait_ge(gathered[u % 2], 16 * TPB * (u // 2))
                for i in range(u * TPB, (u + 1) * TPB):
                    pool.indirect_dma_start(
                        out=back[:, i * P:(i + 1) * P], out_offset=None, in_=m.ys_dram,
                        in_offset=bass.IndirectOffsetOnAxis(ap=m.slots[:, i:i + 1], axis=0)
                    ).then_inc(gathered[u % 2], 16)

        @block.tensor
        def _(pe):
            pe.wait_ge(const_done, 16 * (N_C4 - 1))
            for i in range(3):
                mm = pe.transpose(ps_f[0][:, i * P:(i + 1) * P], w_ld[:, i, :], ident[:, :])
            mm.then_inc(S["wT_ps"], 1)
            pe.wait_ge(S["wT_sb"], 1)

            def project(i, s, bank_free, u):
                for hf in (0, 1):
                    pe.wait_ge(S[bank_free], 2 * (u + 1) + hf + 1)
                    pe.matmul(ps_f[hf][:, :], w_T[:, i, :], xnT[:, hf * 512:(hf + 1) * 512],
                              start=True, stop=True).then_inc(S[s], 1)

            def step(u, half, g, n):
                o = 1 - g
                nxt, cur, prv = (valid(n, k) for k in (1, 0, -1))

                def scores(kt):
                    if kt == 0:
                        pe.wait_ge(S["q_sb"], 2 * u + 2)
                        pe.wait_ge(S["k_sb"], 2 * u + 2)
                    if above_zero(8 * u + kt - 1):
                        pe.wait_ge(S["exp"], 8 * u + kt - 1)
                    for hf in (0, 1):
                        mm = pe.matmul(ps_s[kt % 2][:, hf * 512:(hf + 1) * 512], kT[g][:, kt * P:(kt + 1) * P],
                                       qT[g][:, hf * 512:(hf + 1) * 512], start=True, stop=True)
                    mm.then_inc(S["score"], 1)

                def av(uu, kt):
                    if kt == 0:
                        if above_zero(uu):
                            pe.wait_ge(S["h3"], uu)
                    pe.wait_ge(S["val_n"], 8 * uu + kt + 1)
                    for q in range(TPB):
                        mm = pe.matmul(ps_o[:, q * P:(q + 1) * P], prob[kt % 2][:, q * P:(q + 1) * P],
                                       val_n[kt % 2][:, :], start=(kt == 0 and q % 4 == 0),
                                       stop=(kt == TPB - 1), skip_group_check=True)
                    mm.then_inc(S["av"], 1)

                if cur:
                    scores(0)
                if prv:
                    av(u - 1, 7)
                if cur:
                    scores(1)
                    scores(2)
                    av(u, 0)
                    scores(3)
                    av(u, 1)
                    scores(4)
                    av(u, 2)
                    scores(5)
                if prv:
                    pe.wait_ge(S["xf"], u)
                    if cur:
                        pe.wait_ge(S["v_sb"], 2 * u + 2)
                    if above_zero(u - 1):
                        pe.wait_ge(S["y1"], u - 1)
                    for q in range(TPB):
                        mm = pe.transpose(ps_f[q // 4][:, (q % 4) * P:(q % 4 + 1) * P], xf[:, q, :], ident[:, :])
                    mm.then_inc(S["hT_ps"], 1)
                if cur:
                    av(u, 3)
                    scores(6)
                    av(u, 4)
                if prv:
                    pe.wait_ge(S["mean"], u)
                    pe.matmul(ps_f[0][:, 0:LP], mean[:, :], w_r[:, :], start=True, stop=True).then_inc(S["r_ps"], 1)
                if cur:
                    scores(7)
                if nxt:
                    pe.wait_ge(S["xn"], u + 2)
                    if prv:
                        pe.wait_ge(S["lg"], u)
                    elif cur:
                        pe.wait_ge(S["v_sb"], 2 * u + 2)
                    for hf in (0, 1):
                        for q in range(4):
                            mm = pe.transpose(ps_f[hf][:, q * P:(q + 1) * P], xn[:, 4 * hf + q, :], ident[:, :])
                        mm.then_inc(S["xT_ps"], 1)
                if cur:
                    av(u, 5)
                if nxt:
                    project(0, "q_ps", "xT_sb", u)
                if cur:
                    av(u, 6)
                if nxt:
                    project(1, "k_ps", "q_sb", u)
                if nxt:
                    for hf in (0, 1):
                        pe.wait_ge(S["k_sb"], 2 * (u + 1) + hf + 1)
                        for q in range(4):
                            mm = pe.matmul(ps_f[hf][:, q * P:(q + 1) * P], xnT[:, (4 * hf + q) * P:(4 * hf + q + 1) * P],
                                           w_T[:, 2, :], start=True, stop=True)
                        mm.then_inc(S["v_ps"], 1)
                if prv:
                    pe.wait_ge(we_ld[o], 32 * (half + g))
                    for hf in (0, 1):
                        if nxt:
                            pe.wait_ge(S["v_sb"], 2 * (u + 1) + hf + 1)
                        for q in range(4):
                            mm = pe.matmul(ps_f[hf][:, q * P:(q + 1) * P],
                                           xfT[:, (4 * hf + q) * P:(4 * hf + q + 1) * P], we[o][:, :],
                                           start=True, stop=True)
                    mm.then_inc(S["y_ps"], 1)
            pipeline(pe, -1, B, 2, PAIRS, step)

        @block.scalar
        def _(act):
            act.preload_act_table_set(LN_EXP)
            act.wait_ge(S["wT_ps"], 1)
            act.activation(w_T[:, :, :], ps_f[0][:, 0:3 * P].rearrange("p (a d) -> p a d", a=3),
                           ACT.Copy).then_inc(S["wT_sb"], 1)

            def from_f(dst, filled, emptied, u, func=ACT.Copy, **kw):
                for hf in (0, 1):
                    act.wait_ge(S[filled], 2 * (u + 1) + hf + 1)
                    act.activation(dst[:, hf * 512:(hf + 1) * 512], ps_f[hf][:, :], func,
                                   **kw).then_inc(S[emptied], 1)

            def step(u, half, g, n):
                o = 1 - g
                nxt, cur, prv = (valid(n, k) for k in (1, 0, -1))

                def exp(kt):
                    if above_zero(8 * u + kt - 1):
                        act.wait_ge(S["av"], 8 * u + kt - 1)
                    act.wait_ge(S["bias"], 8 * u + kt + 1)
                    act.activation(prob[kt % 2][:, :], ps_s[kt % 2][:, :], ACT.Exp, scale=SCALE1,
                                   bias=bias_s[:, kt:kt + 1], accum_out=sum_s[:, kt:kt + 1]).then_inc(S["exp"], 1)

                if cur:
                    exp(0)
                    exp(1)
                    exp(2)
                if prv:
                    act.wait_ge(S["st_f"], u)
                    act.activation(lv_f[:, :], mv_f[:, :, 1], ACT.Ln, bias=eps[:, 0:1]).then_inc(S["ln_f"], 1)
                    act.wait_ge(S["ln_f"], u)
                    act.activation(rs_f[:, :], lv_f[:, :], ACT.Exp, scale=-0.5).then_inc(S["rs_f"], 1)
                if cur:
                    exp(3)
                if prv:
                    act.wait_ge(S["nm_f"], u)
                    if above_zero(u - 1):
                        act.wait_ge(S["hT_ps"], u - 1)
                    for q in range(TPB):
                        ins = act.activation(xf[:, q, :], h3c[:, q, :], ACT.Identity, scale=rs_f[:, q:q + 1],
                                             bias=nm_f[:, q:q + 1])
                    ins.then_inc(S["xf"], 1)
                if cur:
                    exp(4)
                if nxt:
                    act.wait_ge(S["st"], u + 2)
                    act.activation(lv[:, :], mv[:, :, 1], ACT.Ln, bias=eps[:, 0:1]).then_inc(S["ln"], 1)
                    act.wait_ge(S["ln"], u + 2)
                    act.activation(rs[:, :], lv[:, :], ACT.Exp, scale=-0.5).then_inc(S["rs"], 1)
                if prv:
                    act.wait_ge(S["hT_ps"], u)
                    if above_zero(u - 1):
                        act.wait_ge(S["y_ps"], u - 1)
                    if above_zero(u - 1):
                        act.wait_ge(S["mean1"], u - 1)
                    for hf in (0, 1):
                        ins = act.activation(xfT[:, hf * 512:(hf + 1) * 512], ps_f[hf][:, :], ACT.Identity,
                                             accum_out=xf_sum[:, hf:hf + 1])
                    ins.then_inc(S["hT_sb"], 1)
                if cur:
                    exp(5)
                if nxt:
                    act.wait_ge(S["nm"], u + 2)
                    if above_zero(2 * u + 2):
                        act.wait_ge(S["xT_ps"], 2 * u + 2)
                    for q in range(TPB):
                        ins = act.activation(xn[:, q, :], tile(h, u + 1, q), ACT.Identity, scale=rs[:, q:q + 1],
                                             bias=nm[:, q:q + 1])
                    ins.then_inc(S["xn"], 1)
                if cur:
                    exp(6)
                if prv:
                    act.wait_ge(S["lg_top"], u)
                    act.activation(ex[:, :], lg[:, :], ACT.Exp, bias=lg_top[:, 0:1],
                                   accum_out=ex_sum[:, 0:1]).then_inc(S["ex"], 1)
                if nxt:
                    from_f(xnT, "xT_ps", "xT_sb", u)
                if cur:
                    exp(7)
                if nxt:
                    from_f(qT[o], "q_ps", "q_sb", u, ACT.Identity, bias=b_q[:, 0:1])
                if nxt:
                    from_f(kT[o], "k_ps", "k_sb", u, ACT.Identity, bias=b_k[:, 0:1])
            pipeline(act, -1, B, 2, PAIRS, step)

        @block.vector
        def _(dve):
            dve.wait_ge(const_done, 16 * (N_C4 - 1))

            def step(u, half, g, n):
                o = 1 - g
                nxt, cur, prv = (valid(n, k) for k in (1, 0, -1))

                def tops(kt):
                    dve.wait_ge(S["score"], 8 * u + kt + 1)
                    if above_zero(8 * u + kt - 7):
                        dve.wait_ge(S["exp"], 8 * u + kt - 7)
                    dve.tensor_reduce(top_s[:, kt:kt + 1], ps_s[kt % 2][:, :], AXX, ALU.max).then_inc(S["top"], 1)
                    dve.wait_ge(S["top"], 8 * u + kt + 1)
                    dve.tensor_scalar(bias_s[:, kt:kt + 1], top_s[:, kt:kt + 1], -SCALE1, None,
                                      ALU.mult).then_inc(S["bias"], 1)

                def values(kt):
                    dve.wait_ge(S["exp"], 8 * u + kt + 1)
                    dve.reciprocal(inv_s[:, kt:kt + 1], sum_s[:, kt:kt + 1]).then_inc(S["inv"], 1)
                    dve.wait_ge(S["inv"], 8 * u + kt + 1)
                    if above_zero(8 * u + kt - 1):
                        dve.wait_ge(S["av"], 8 * u + kt - 1)
                    dve.tensor_scalar(val_n[kt % 2][:, :], val[g][:, kt, :], inv_s[:, kt:kt + 1], None,
                                      ALU.mult).then_inc(S["val_n"], 1)

                if cur:
                    tops(0)
                if prv:
                    dve.wait_ge(S["av"], 8 * u)
                    if above_zero(u - 1):
                        dve.wait_ge(S["out"], u - 1)
                    for hf in (0, 1):
                        ins = dve.tensor_tensor(h3c[:, 4 * hf:4 * hf + 4, :].rearrange("p a d -> p (a d)"),
                                                ps_o[:, hf * 512:(hf + 1) * 512],
                                                h[:, bass.ds((u - 1) * SEQ + hf * 512, 512)], ALU.add)
                    ins.then_inc(S["h3"], 1)
                if cur:
                    tops(1)
                    values(0)
                if prv:
                    dve.wait_ge(S["h3"], u)
                    dve.sem_inc(passed, 1)
                    for q in range(TPB):
                        ins = dve.bn_stats(stat_f[:, q, :], h3c[:, q, :])
                    ins.then_inc(S["bn_f"], 1)
                if cur:
                    tops(2)
                    values(1)
                if prv:
                    dve.wait_ge(S["bn_f"], u)
                    dve.sem_inc(passed, 1)
                    for q in range(TPB):
                        ins = dve.bn_aggr(mv_f[:, q, :], stat_f[:, q, :])
                    ins.then_inc(S["st_f"], 1)
                if nxt:
                    dve.wait_ge(gathered[o], 16 * TPB * (half + g + 1))
                    for q in range(TPB):
                        ins = dve.scalar_tensor_tensor(tile(h, u + 1, q), tile(back, u + 1, q),
                                                       m.gate[:, bass.ds((u + 1) * TPB + q, 1)],
                                                       tile(h, u + 1, q), ALU.mult, ALU.add)
                    ins.then_inc(S["h2"], 1)
                if cur:
                    tops(3)
                if prv:
                    dve.wait_ge(S["rs_f"], u)
                    dve.scalar_tensor_tensor(nm_f[:, :], mv_f[:, :, 0], -1.0, rs_f[:, :], ALU.mult,
                                             ALU.mult).then_inc(S["nm_f"], 1)
                if cur:
                    values(2)
                if nxt:
                    dve.wait_ge(S["h2"], u + 2)
                    dve.sem_inc(passed, 1)
                    for q in range(TPB):
                        ins = dve.bn_stats(stat[:, q, :], tile(h, u + 1, q))
                    ins.then_inc(S["bn"], 1)
                if cur:
                    tops(4)
                    values(3)
                if nxt:
                    dve.wait_ge(S["bn"], u + 2)
                    dve.sem_inc(passed, 1)
                    for q in range(TPB):
                        ins = dve.bn_aggr(mv[:, q, :], stat[:, q, :])
                    ins.then_inc(S["st"], 1)
                if cur:
                    tops(5)
                if nxt:
                    dve.wait_ge(S["rs"], u + 2)
                    dve.scalar_tensor_tensor(nm[:, :], mv[:, :, 0], -1.0, rs[:, :], ALU.mult,
                                             ALU.mult).then_inc(S["nm"], 1)
                if cur:
                    values(4)
                if prv:
                    dve.wait_ge(S["hT_sb"], u)
                    dve.tensor_tensor(mean1[:, :], xf_sum[:, 0:1], xf_sum[:, 1:2], ALU.add).then_inc(S["mean1"], 1)
                    dve.wait_ge(S["mean1"], u)
                    dve.tensor_scalar(mean[:, :], ones[:, :], mean1[:, 0:1], 1.0 / SEQ, ALU.mult,
                                      ALU.mult).then_inc(S["mean"], 1)
                if cur:
                    tops(6)
                if prv:
                    dve.wait_ge(S["r_ps"], u)
                    dve.tensor_tensor(lg[:, :], ps_f[0][:, 0:E1], b_r[:, :], ALU.add).then_inc(S["lg"], 1)
                    dve.wait_ge(S["lg"], u)
                    dve.tensor_reduce(lg_top[:, :], lg[:, :], AXX, ALU.max, negate=True).then_inc(S["lg_top"], 1)
                if cur:
                    values(5)
                    tops(7)
                    values(6)
                if prv:
                    dve.wait_ge(S["ex"], u)
                    dve.sem_inc(passed, 1)
                    dve.max(ex_top[:, :], ex[:, :]).then_inc(S["ex_top"], 1)
                    dve.wait_ge(S["ex_top"], u)
                    dve.sem_inc(passed, 1)
                    dve.max_index(ex_at[:, :], ex_top[:, :], ex[:, :]).then_inc(S["ex_at"], 1)
                    dve.reciprocal(gate[o][:, :], ex_sum[:, :]).then_inc(S["gate"], 1)
                if cur:
                    values(7)
                if nxt:
                    for hf in (0, 1):
                        dve.wait_ge(S["v_ps"], 2 * (u + 1) + hf + 1)
                        dve.tensor_tensor(val[o][:, 4 * hf:4 * hf + 4, :],
                                          ps_f[hf][:, :].rearrange("p (a d) -> p a d", a=4),
                                          b_v[:, :].unsqueeze(1).to_broadcast([P, 4, P]),
                                          ALU.add).then_inc(S["v_sb"], 1)
                if prv:
                    dve.wait_ge(S["y_ps"], u)
                    for hf in (0, 1):
                        ins = dve.tensor_tensor(y1[:, hf * 512:(hf + 1) * 512].rearrange("p (a d) -> p a d", a=4),
                                                ps_f[hf][:, :].rearrange("p (a d) -> p a d", a=4),
                                                be[o][:, :].unsqueeze(1).to_broadcast([P, 4, P]), ALU.add)
                    ins.then_inc(S["y1"], 1)
                    dve.wait_ge(S["y1"], u)
                    dve.wait_ge(S["gate"], u)
                    if above_zero(16 * (half + g - 1)):
                        dve.wait_ge(o_st[o], 16 * (half + g - 1))
                    dve.scalar_tensor_tensor(o_sb[o][:, :, :].rearrange("p a d -> p (a d)"), y1[:, :],
                                             gate[o][:, 0:1], h3c[:, :, :].rearrange("p a d -> p (a d)"),
                                             ALU.mult, ALU.add).then_inc(S["out"], 1)
            pipeline(dve, -1, B, 2, PAIRS, step)


_INS = ["x", "L0_tok_W", "L0_attn_W_Q", "L0_attn_W_K", "L0_attn_W_V", "L0_attn_W_G", "L0_attn_W_O",
        "L0_attn_gn_weight", "L0_attn_gn_bias", "L0_ffn_w_gating", "L0_ffn_gamma", "L0_ffn_w1",
        "L0_ffn_w2", "L1_attn_Wq", "L1_attn_bq", "L1_attn_Wk", "L1_attn_bk", "L1_attn_Wv",
        "L1_attn_bv", "L1_ffn_Wg", "L1_ffn_bg", "L1_ffn_We", "L1_ffn_be"]


def kernel(**inputs):
    import concourse.bacc as bacc
    from concourse.bass_utils import run_bass_kernel_spmd

    nc = bacc.Bacc("TRN2", target_bir_lowering=False, num_devices=1)
    arrays, t, cst = {}, {}, {}
    for name in _INS:
        a = np.ascontiguousarray(inputs[name])
        arrays["in_" + name] = a
        t[name] = nc.dram_tensor("in_" + name, a.shape, mybir.dt.from_np(a.dtype), kind="ExternalInput").ap()
    for name, a in constants().items():
        arrays["const_" + name] = a
        cst[name] = nc.dram_tensor("const_" + name, a.shape, mybir.dt.from_np(a.dtype), kind="ExternalInput").ap()
    out = nc.dram_tensor("out", (B, SEQ, P), F32, kind="ExternalOutput").ap()
    tower(nc, t, cst, out)
    r = run_bass_kernel_spmd(nc, [arrays], core_ids=[0])
    return r.results[0]["out"]
```

```python
import math
from contextlib import ExitStack

import numpy as np

import concourse.bass as bass
from concourse import mybir
from concourse.alu_op_type import AluOpType as ALU

ACT = mybir.ActivationFunctionType
F32 = mybir.dt.float32
F32R = mybir.dt.float32r
BF16 = mybir.dt.bfloat16
I32 = mybir.dt.int32
U32 = mybir.dt.uint32
AXX = mybir.AxisListType.X

P = 128
B, SEQ, F_IN = 8, 1024, 29
TPB = SEQ // P
TILES = B * TPB
GT = 4
GROUPS = TILES // GT
GN = GT * P
H, DH = 8, 16
FX = GT * F_IN
E0, HID = 6, 512
HB = HID // P
ET = 256
NET = TILES * P // ET + E0 - 1
E1 = 16
LP = 96
LN_EPS = 1e-5
GATE_EPS = 1e-9
SCALE1 = float(1.0 / (np.sqrt(np.float32(P)) + np.float32(1e-6)))
LN_EXP = "natural_log_exp_and_others"
NO_EXPERT = -3e38
CAP = TILES * P + ET
SPARE = NET - TILES * P // ET
ROWS = E0 * CAP + SPARE * ET
N_EXPERT = 2 * E0 + 1
N_FIRST = GT + 1
N_CONST = 22
POS0 = GT * LP
assert NET * ET >= TILES * P + (E0 - 1) * (ET - 1)
assert POS0 + (GT + 1) * E0 <= 512


def constants():
    pos = np.arange(SEQ, dtype=np.float32)[:, None]
    div = np.exp(np.arange(0, P, 2, dtype=np.float32) * (-math.log(10000.0) / P))
    pe = np.zeros((SEQ, P), np.float32)
    pe[:, 0::2] = np.sin(pos * div)
    pe[:, 1::2] = np.cos(pos * div)
    gam = 1.0 - np.exp2(-5.0 - np.arange(H, dtype=np.float64))
    t = np.arange(P)
    diff = t[None, :] - t[:, None]
    head = np.arange(P) // DH
    same = (head[:, None] == head[None, :]).astype(np.float64)
    dec = np.where(diff[:, None, :] >= 0, gam[None, :, None] ** np.maximum(diff, 0)[:, None, :], 0.0)
    out = {
        "pe": pe.reshape(TPB, P, P).transpose(1, 0, 2),
        "decay": dec / math.sqrt(DH),
        "q_decay": gam[head][:, None] ** (t[None, :] + 1) / math.sqrt(DH),
        "k_decay": gam[head][None, :] ** (P - 1 - t[:, None]),
        "state_decay": (gam[head] ** P)[:, None],
        "head_mask": (head[:, None] == np.arange(H)[None, :]),
        "same_head": same,
        "center": np.eye(P) - same / DH,
        "average": same / DH,
        "ident": np.eye(P),
        "before": t[:, None] < t[None, :],
        "expert_no": np.broadcast_to(np.arange(E0)[None, :], (P, E0)),
        "tile_no": np.broadcast_to(np.arange(NET)[None, :], (P, NET)),
        "region": np.broadcast_to(CAP * np.arange(E0)[None, :], (P, E0)),
    }
    return {k: np.ascontiguousarray(v, dtype=np.float32) for k, v in out.items()}


def above_zero(count):
    return not isinstance(count, int) or count > 0


def pipeline(eng, first, last, body_from, body_pairs, step):
    for n in range(first, body_from):
        step(n, n // 2, n % 2, n)
    with eng.Fori(0, body_pairs) as k:
        step(2 * k + body_from, k + body_from // 2, 0, None)
        step(2 * k + body_from + 1, k + body_from // 2, 1, None)
    for n in range(body_from + 2 * body_pairs, last + 1):
        step(n, n // 2, n % 2, n)


class Shared:
    pass


def tower(nc, t, cst, out):
    with ExitStack() as ctx:
        def sb(name, shape, dt=F32):
            return ctx.enter_context(nc.sbuf_tensor(name, shape, dt))

        m = Shared()
        m.xs_dram = nc.dram_tensor("xs_dram", (ROWS, P), F32, kind="Internal").ap()
        m.ys_dram = nc.dram_tensor("ys_dram", (NET * ET, P), F32, kind="Internal").ap()
        m.ident = sb("ident", [P, P])
        m.ones = sb("ones", [P, P])
        m.eps = sb("eps", [P, 1])
        m.w1 = sb("w1", [P, E0 * HID])
        m.w2 = sb("w2", [P, E0 * HID])
        m.h = sb("h", [P, TILES * P])
        m.logits = sb("logits", [P, TILES, 8])
        m.top = sb("top", [P, TILES, 8])
        m.choice = sb("choice", [P, TILES])
        m.row = sb("row", [P, TILES])
        m.slots = sb("slots", [P, TILES], U32)
        m.shift = sb("shift", [P, E0])
        m.gate = sb("gate", [P, TILES])
        m.next_row = sb("next_row", [P, E0])
        m.zeros = sb("zeros", [P, SPARE * ET // P, P])
        m.tile_e = sb("tile_e", [P, NET], I32)
        m.tile_row = sb("tile_row", [P, NET], I32)
        m.passed = ctx.enter_context(nc.semaphore("passed"))
        m.s_experts = ctx.enter_context(nc.semaphore("s_experts"))
        m.s_scattered = [ctx.enter_context(nc.semaphore(f"s_scattered{i}")) for i in (0, 1)]
        m.s_padded = ctx.enter_context(nc.semaphore("s_padded"))
        for phase in (phase1, phase2, phase3):
            with ExitStack() as ph:
                phase(nc, ctx, ph, m, t, cst, out)


def phase1(nc, ctx, ph, m, t, cst, out):
    h, logits, top, ident, eps = m.h, m.logits, m.top, m.ident, m.eps

    def sb(name, shape, dt=F32):
        return ph.enter_context(nc.sbuf_tensor(name, shape, dt))

    def psum(name, shape, dt=F32):
        return ph.enter_context(nc.psum_tensor(name, shape, dt))

    def sem(name):
        return ctx.enter_context(nc.semaphore(name))

    pe_c = sb("pe_c", [P, TPB, P])
    decay = sb("decay", [P, H, P])
    q_decay = sb("q_decay", [P, P])
    k_decay = sb("k_decay", [P, P])
    state_decay = sb("state_decay", [P, 1])
    head_mask = sb("head_mask", [P, H])
    same_head = sb("same_head", [P, P])
    center = sb("center", [P, P])
    average = sb("average", [P, P])
    w_tok = sb("w_tok", [P, GT, P])
    wq, wk, wg, wo = (sb(n, [P, P]) for n in ("wq", "wk", "wg", "wo"))
    wv = sb("wv", [P, P])
    gn_w = sb("gn_w", [P, 1])
    gn_b = sb("gn_b", [P, 1])
    wgate = sb("wgate", [P, LP])
    gamma_b = sb("gamma_b", [P, P])
    before = sb("before", [P, P])
    before_bf = sb("before_bf", [P, P], BF16)
    ones_bf = sb("ones_bf", [P, P], BF16)
    expert_no = sb("expert_no", [P, E0])

    x_sb = [sb(f"x_sb{i}", [P, GT, F_IN]) for i in (0, 1)]
    xT_sb = sb("xT_sb", [P, P])
    stat1, stat2 = (sb(f"stat{i}", [P, GT, 6]) for i in (1, 2))
    mv1, mv2 = (sb(f"mv{i}", [P, GT, 2]) for i in (1, 2))
    lv1, lv2, lv3 = (sb(f"lv{i}", [P, GT]) for i in (1, 2, 3))
    r1, r2, r3 = (sb(f"r{i}", [P, GT]) for i in (1, 2, 3))
    nm1, nm2 = (sb(f"nm{i}", [P, GT]) for i in (1, 2))
    inv2 = sb("inv2", [P, GT])
    v3 = sb("v3", [P, GT])
    xn = sb("xn", [P, GT, P])
    xnT = [sb(f"xnT{i}", [P, GN]) for i in (0, 1)]
    x_hi, x_lo = (sb(n, [P, GN], F32R) for n in ("p1x_hi", "p1x_lo"))
    w_hi = [sb(f"p1w_hi{i}", [P, P], F32R) for i in range(3)]
    w_lo = [sb(f"p1w_lo{i}", [P, P], F32R) for i in range(3)]
    qT = [sb(f"qT{i}", [P, GN]) for i in (0, 1)]
    kT = [sb(f"kT{i}", [P, GN]) for i in (0, 1)]
    gT = [sb(f"gT{i}", [P, GN]) for i in (0, 1)]
    q_in = [sb(f"q_in{i}", [P, GT, P]) for i in (0, 1)]
    q_head = [sb(f"q_head{i}", [P, H, P]) for i in (0, 1)]
    k_out = [sb(f"k_out{i}", [P, P]) for i in (0, 1)]
    v_pad = [sb(f"v_pad{i}", [P, H // 2, 4, DH]) for i in (0, 1)]
    prob = [sb(f"prob{i}", [P, H, P]) for i in (0, 1)]
    state = [sb(f"state{i}", [P, P]) for i in (0, 1)]
    s_new = sb("s_new", [P, P])
    wv_T = sb("wv_T", [P, P])
    cen = sb("cen", [P, GN])
    sq = sb("sq", [P, GN])
    lvar = sb("lvar", [P, GN])
    rstd = sb("rstd", [P, GN])
    t1 = sb("t1", [P, GN])
    t2 = sb("t2", [P, GN])
    act_T = sb("act_T", [P, GN])
    xn2 = sb("xn2", [P, GT, P])
    x2T = sb("x2T", [P, GN])
    lg = sb("lg", [P, GT, 8])
    lg_top = sb("lg_top", [P, GT, 8])
    lg_at = sb("lg_at", [P, GT, 8], U32)
    choice = sb("choice_g", [P, GT])
    onehot = sb("onehot", [P, GT + 1, E0], BF16)
    row_e = sb("row_e", [P, GT, E0])
    row_1 = sb("row_1", [P, GT, E0])
    row_f = sb("row_f", [P, GT])
    row_i = [sb(f"row_i{i}", [P, GT], U32) for i in (0, 1)]
    send = [sb(f"send{i}", [P, GT, P]) for i in (0, 1)]
    xn3 = sb("xn3", [P, GT, P])

    ps_s = [psum(f"ps_s{i}", [P, GN]) for i in (0, 1)]
    ps_j = [psum(f"ps_j{i}", [P, GN]) for i in (0, 1)]
    ps_r = psum("ps_r", [P, GN])
    ps_g = psum("ps_g", [P, GN])
    ps_m = [psum(f"ps_m{i}", [P, GN]) for i in (0, 1)]

    names = ("xt_ps xt_sb h0_ps h0 bn1 st1 ln1 r1 nm1 xn xnT_ps x_hi xnT_sb x_lo w_parts proj_ps proj_sb q_in q_head "
             "kv_ps k_out v_pad score prob pv st_ps tmp state cen var_ps lvar rstd "
             "t1 t2 silu wo_ps h1 bn2 st2 ln2 r2 nm2 inv2 xn2 x2T_ps x2T_sb v3 ln3 r3 xn3 xnn "
             "logit_ps logit top top_i kept wv_ps wv_sb choice onehot pos_ps row_e next_row row_1 row_f slots").split()
    S = {n: sem("p1_" + n) for n in names}

    tile_no = sb("tile_no", [P, NET])
    region = sb("region", [P, E0])
    end_i = sb("end_i", [P, E0], I32)
    n_f = sb("n_f", [P, E0])
    n_i = sb("n_i", [P, E0], I32)
    n_tiles_i = sb("n_tiles_i", [P, E0], I32)
    n_tiles = sb("n_tiles", [P, E0])
    ends = sb("ends", [P, E0])
    starts = sb("starts", [P, E0])
    skip = sb("skip", [P, E0])
    past = sb("past", [P, NET, E0])
    skips = sb("skips", [P, NET, E0])
    tile_f = sb("tile_f", [P, NET])
    tile_off = sb("tile_off", [P, NET])
    row_s = sb("row_s", [P, NET])
    tile_row_f = sb("row_f2", [P, NET])
    diff = sb("diff", [P, TILES, E0])
    expd = sb("expd", [P, TILES, E0])
    total = sb("total", [P, TILES])
    d2 = sb("d2", [P, TILES])
    e2 = sb("e2", [P, TILES])
    den = sb("den", [P, TILES])
    ended, differences, exps, steps = (
        sem("p1_" + n) for n in ("ended", "differences", "exps", "steps"))


    def valid(n, k):
        return n is None or 0 <= n + k < GROUPS

    def tile(buf, u, t):
        return buf[:, bass.ds(u * GN + t * P, P)]

    x_t = t["x"].rearrange("b hh w f -> (b hh w) f").rearrange("(t p) f -> p t f", p=P)
    first_done = sem("p1_first")
    pos_done = sem("p1_pos")
    const_done = sem("p1_const")
    zero_first = sem("p1_zero_first")
    zero_done = sem("p1_zero")
    passed = m.passed
    x_ld = [sem(f"p1_x_ld{i}") for i in (0, 1)]

    with nc.Block() as block:
        @block.sync
        def _(sp):
            consts = [(decay, cst["decay"]), (q_decay, cst["q_decay"]),
                      (k_decay, cst["k_decay"]), (state_decay, cst["state_decay"]),
                      (head_mask, cst["head_mask"]), (same_head, cst["same_head"]),
                      (center, cst["center"]), (average, cst["average"]),
                      (wq, t["L0_attn_W_Q"]), (wk, t["L0_attn_W_K"]), (wg, t["L0_attn_W_G"]),
                      (wo, t["L0_attn_W_O"]), (before, cst["before"]), (expert_no, cst["expert_no"]),
                      (m.next_row, cst["region"]), (region, cst["region"]), (tile_no, cst["tile_no"])]
            assert N_CONST == len(consts) + 5
            sp.dma_start(ident[:, :], cst["ident"]).then_inc(first_done, 16)
            for n in (0, 1):
                sp.dma_start(x_sb[n][:, :, :], x_t[:, GT * n:GT * n + GT, :]).then_inc(x_ld[n], 16)
            sp.wait_ge(zero_first, 1)
            for c in range(GT):
                sp.dma_start(w_tok[c * F_IN:(c + 1) * F_IN, c, :], t["L0_tok_W"]).then_inc(first_done, 16)
            sp.dma_start(pe_c[:, :, :], cst["pe"]).then_inc(pos_done, 16)
            for dst, src in consts:
                dst = dst[:, :, :] if len(dst.shape) == 3 else dst[:, :]
                sp.dma_start(dst, src).then_inc(const_done, 16)
            sp.dma_start(wv[:, :], t["L0_attn_W_V"]).then_inc(const_done, 16)
            sp.dma_start(gn_w[:, :], t["L0_attn_gn_weight"].unsqueeze(1)).then_inc(const_done, 16)
            sp.dma_start(gn_b[:, :], t["L0_attn_gn_bias"].unsqueeze(1)).then_inc(const_done, 16)
            sp.dma_start(gamma_b[:, :], t["L0_ffn_gamma"].partition_broadcast(P)).then_inc(const_done, 16)
            sp.wait_ge(zero_done, 1)
            sp.dma_start(wgate[:, 0:E0], t["L0_ffn_w_gating"]).then_inc(const_done, 16)
            for e in range(E0):
                sp.dma_start(m.w1[:, e * HID:(e + 1) * HID], t["L0_ffn_w1"][e]).then_inc(m.s_experts, 16)
                sp.dma_start(m.w2[:, e * HID:(e + 1) * HID].rearrange("p (k d) -> p k d", k=HB),
                             t["L0_ffn_w2"][e].rearrange("(k p) d -> p k d", p=P)).then_inc(m.s_experts, 16)
            sp.dma_start(m.xs_dram[E0 * CAP:ROWS, :].rearrange("(a p) d -> p a d", p=P),
                         m.zeros[:, :, :]).then_inc(m.s_experts, 16)

            def step(u, half, g, n):
                if n is not None and (n < 1 or n >= GROUPS - 1):
                    return
                sp.wait_ge(S["xt_ps"], u)
                sp.dma_start(x_sb[1 - g][:, :, :], x_t[:, bass.ds(GT * (u + 1), GT), :]).then_inc(x_ld[1 - g], 16)
            pipeline(sp, -1, GROUPS + 1, 2, (GROUPS - 4) // 2, step)
            sp.wait_ge(ended, 1)
            for e in range(E0):
                end = sp.value_load(end_i[0:1, e:e + 1], min_val=e * CAP, max_val=e * CAP + TILES * P)
                sp.dma_start(m.xs_dram[bass.ds(end, ET), :].rearrange("(a p) d -> p a d", p=P),
                             m.zeros[:, 0:ET // P, :]).then_inc(m.s_padded, 16)

        @block.gpsimd
        def _(pool):
            for dst in (w_tok, xT_sb):
                pool.memset(dst[:], 0.0)
            pool.memset(eps[:, :], LN_EPS)
            pool.drain().then_inc(zero_first, 1)
            for dst in (wgate, v_pad[0], v_pad[1], m.zeros, onehot):
                pool.memset(dst[:], 0.0)
            pool.memset(ones_bf[:, :], 1.0)
            pool.memset(lg[:, :, :], NO_EXPERT)
            pool.memset(m.ones[:, :], 1.0)
            pool.drain().then_inc(zero_done, 1)
            pool.wait_ge(const_done, 16 * N_CONST)

            def scatter(u, o, c):
                if c == 0:
                    pool.wait_ge(S["slots"], u - 2)
                    pool.sem_inc(passed, 1)
                    pool.wait_ge(S["xnn"], u - 2)
                    pool.sem_inc(passed, 1)
                pool.indirect_dma_start(
                    out=m.xs_dram, out_offset=bass.IndirectOffsetOnAxis(ap=row_i[o][:, c:c + 1], axis=0),
                    in_=send[o][:, c, :], in_offset=None).then_inc(m.s_scattered[o], 16)

            def step(u, half, g, n):
                if valid(n, 0):
                    for c in range(GT):
                        if c == 0:
                            pool.wait_ge(S["proj_sb"], 3 * u + 1)
                        if above_zero(8 * u + 2 * c - 2):
                            pool.wait_ge(S["score"], 8 * u + 2 * c - 2)
                        pool.tensor_tensor(
                            q_head[c % 2][:, :, :],
                            qT[g][:, c * P:(c + 1) * P].unsqueeze(1).to_broadcast([P, H, P]),
                            head_mask[:, :].unsqueeze(2).to_broadcast([P, H, P]),
                            ALU.mult).then_inc(S["q_head"], 1)
                        if c == 1:
                            pool.tensor_tensor(
                                q_in[g][:, :, :], qT[g][:, :].rearrange("p (c t) -> p c t", c=GT),
                                q_decay[:, :].unsqueeze(1).to_broadcast([P, GT, P]),
                                ALU.mult).then_inc(S["q_in"], 1)
                        if valid(n, -3) and c > 0:
                            scatter(u, 1 - g, c - 1)
                    if valid(n, -3):
                        scatter(u, 1 - g, GT - 1)
                if valid(n, -3) and not valid(n, 0):
                    for c in range(GT):
                        scatter(u, 1 - g, c)
                if valid(n, -2):
                    pool.wait_ge(S["r3"], u - 1)
                    pool.tensor_tensor(xn3[:, :, :], xn2[:, :, :], r3[:, :].unsqueeze(2).to_broadcast([P, GT, P]),
                                       ALU.mult).then_inc(S["xn3"], 1)
                    pool.wait_ge(S["xn3"], u - 1)
                    if above_zero(16 * GT * (half - 1)):
                        pool.wait_ge(m.s_scattered[g], 16 * GT * (half - 1))
                    pool.tensor_tensor(send[g][:, :, :], xn3[:, :, :], gamma_b[:, :].unsqueeze(1).to_broadcast([P, GT, P]),
                                       ALU.mult).then_inc(S["xnn"], 1)
            pipeline(pool, -1, GROUPS + 2, 4, (GROUPS - 6) // 2, step)

        @block.tensor
        def _(pe):
            pe.wait_ge(first_done, 16 * N_FIRST)

            def kv(u, g, c):
                if c == 0:
                    pe.wait_ge(S["wv_sb"], 2)
                    pe.wait_ge(S["xnT_sb"], u + 1)
                    pe.wait_ge(S["proj_sb"], 3 * u + 1)
                if above_zero(4 * u + c - 1):
                    pe.wait_ge(S["v_pad"], 4 * u + c - 1)
                if above_zero(4 * u + c - 1):
                    pe.wait_ge(S["tmp"], 4 * u + c - 1)
                pe.matmul(ps_j[c % 2][:, P:2 * P], xnT[g][:, c * P:(c + 1) * P], wv[:, :], start=True, stop=True)
                if c == 0:
                    pe.wait_ge(S["proj_sb"], 3 * u + 2)
                pe.transpose(ps_j[c % 2][:, 0:P], kT[g][:, c * P:(c + 1) * P], ident[:, :]).then_inc(S["kv_ps"], 1)

            def scores(u, g, c):
                pe.wait_ge(S["q_head"], 4 * u + c + 1)
                for half in (0, 1):
                    if above_zero(8 * u + 2 * c + half - 1):
                        pe.wait_ge(S["prob"], 8 * u + 2 * c + half - 1)
                    pe.matmul(ps_s[half][:, :], kT[g][:, c * P:(c + 1) * P],
                              q_head[c % 2][:, 4 * half:4 * half + 4, :],
                              start=True, stop=True).then_inc(S["score"], 1)

            def state_mm(u, c, after_proj):
                pe.wait_ge(S["k_out"], 4 * u + c + 1)
                pe.wait_ge(S["v_pad"], 4 * u + c + 1)
                if above_zero(4 * u + c - 1):
                    pe.wait_ge(S["tmp"], 4 * u + c - 1)
                if after_proj:
                    pe.wait_ge(S["proj_sb"], 3 * (u + 1) + 2)
                pe.matmul(ps_j[c % 2][:, 2 * P:3 * P], k_out[c % 2][:, :],
                          v_pad[c % 2][:, :, 0:4:3, :], start=True, stop=True).then_inc(S["st_ps"], 1)

            def pv(u, g, c):
                if c == 0:
                    if above_zero(u):
                        pe.wait_ge(S["cen"], u)
                    pe.wait_ge(S["q_in"], u + 1)
                pe.wait_ge(S["prob"], 8 * u + 2 * c + 2)
                inter = not (g == 0 and c == 0)
                for r in (0, 1):
                    for pr in range(H // 2):
                        mm = pe.matmul(ps_r[32 * pr:32 * pr + 32, c * P:(c + 1) * P],
                                  v_pad[c % 2][:, pr, 2 * r:2 * r + 2, :],
                                  prob[c % 2][:, 2 * pr + r, :],
                                  start=(r == 0), stop=(r == 1 and not inter),
                                  skip_group_check=True)
                if inter:
                    pe.wait_ge(S["state"], 4 * u + c)
                    mm = pe.matmul(ps_r[:, c * P:(c + 1) * P], state[c % 2][:, :], q_in[g][:, c, :],
                                   start=False, stop=True, skip_group_check=True)
                mm.then_inc(S["pv"], 1)

            def step(u, half, g, n):
                o = 1 - g
                nxt, cur, prv, prv2 = (valid(n, k) for k in (1, 0, -1, -2))
                if cur:
                    kv(u, g, 0)
                if nxt:
                    pe.wait_ge(x_ld[o], 16 * (half + g + 1))
                    if above_zero(u - 2):
                        pe.wait_ge(S["next_row"], u - 2)
                    pe.transpose(ps_m[0][0:FX, 0:P], x_sb[o][:, :, :].rearrange("p t f -> p (t f)"),
                                 ident[:, :]).then_inc(S["xt_ps"], 1)
                if prv:
                    state_mm(u - 1, 3, cur)
                    pv(u - 1, o, 3)
                if cur:
                    scores(u, g, 0)
                if nxt:
                    pe.wait_ge(S["xt_sb"], u + 2)
                    if above_zero(3 * u + 3):
                        pe.wait_ge(S["proj_sb"], 3 * u + 3)
                    pe.matmul(ps_m[1][:, :], xT_sb[:, :], w_tok[:, :, :],
                              start=True, stop=True).then_inc(S["h0_ps"], 1)
                if cur:
                    kv(u, g, 1)
                    state_mm(u, 0, False)
                    scores(u, g, 1)
                if prv:
                    pe.wait_ge(S["cen"], u)
                    if above_zero(u - 1):
                        pe.wait_ge(S["h1"], u - 1)
                    pe.matmul(ps_g[:, :], average[:, :], sq[:, :], start=True, stop=True).then_inc(S["var_ps"], 1)
                if cur:
                    pv(u, g, 0)
                if cur:
                    kv(u, g, 2)
                    state_mm(u, 1, False)
                    scores(u, g, 2)
                if prv2:
                    pe.wait_ge(S["xn2"], u - 1)
                    if above_zero(u - 2):
                        pe.wait_ge(S["next_row"], u - 2)
                    if nxt:
                        pe.wait_ge(S["xt_sb"], u + 2)
                    for t in range(GT):
                        mm = pe.transpose(ps_m[0][:, t * P:(t + 1) * P], xn2[:, t, :], ident[:, :])
                    mm.then_inc(S["x2T_ps"], 1)
                if cur:
                    pv(u, g, 1)
                if cur:
                    kv(u, g, 3)
                    state_mm(u, 2, False)
                    scores(u, g, 3)
                if prv2:
                    pe.wait_ge(S["x2T_sb"], u - 1)
                    for t in range(GT):
                        mm = pe.matmul(ps_m[0][:, t * LP:(t + 1) * LP], x2T[:, t * P:(t + 1) * P],
                                       wgate[:, :], start=True, stop=True)
                    mm.then_inc(S["logit_ps"], 1)
                if nxt:
                    pe.wait_ge(S["xn"], u + 2)
                    for t in range(GT):
                        mm = pe.transpose(ps_m[1][:, t * P:(t + 1) * P], xn[:, t, :], ident[:, :])
                    mm.then_inc(S["xnT_ps"], 1)
                if cur:
                    pv(u, g, 2)
                if prv:
                    pe.wait_ge(S["silu"], u)
                    for t in range(GT):
                        mm = pe.matmul(ps_g[:, t * P:(t + 1) * P], act_T[:, t * P:(t + 1) * P], wo[:, :],
                                       start=True, stop=True)
                    mm.then_inc(S["wo_ps"], 1)
                if n == -1:
                    pe.wait_ge(const_done, 16 * N_CONST)
                    pe.transpose(ps_g[:, 0:P], wv[:, :], ident[:, :]).then_inc(S["wv_ps"], 1)
                    pe.wait_ge(S["wv_sb"], 1)
                    pe.matmul(ps_g[:, P:2 * P], wv_T[:, :], center[:, :], start=True,
                              stop=True).then_inc(S["wv_ps"], 1)
                if nxt:
                    def part(bank, w, x, first, last):
                        return pe.matmul(bank[:, :], w[:, :], x[:, :], start=first, stop=last)
                    pe.wait_ge(S["w_parts"], 2)
                    pe.wait_ge(S["x_hi"], u + 2)
                    if above_zero(4 * u + 3):
                        pe.wait_ge(S["tmp"], 4 * u + 3)
                    part(ps_j[0], w_hi[0], x_hi, True, False)
                    part(ps_j[0], w_lo[0], x_hi, False, False)
                    if above_zero(4 * u + 4):
                        pe.wait_ge(S["k_out"], 4 * u + 4)
                    if above_zero(4 * u + 4):
                        pe.wait_ge(S["v_pad"], 4 * u + 4)
                    part(ps_j[1], w_hi[1], x_hi, True, False)
                    part(ps_j[1], w_lo[1], x_hi, False, False)
                    pe.wait_ge(S["x_lo"], u + 2)
                    part(ps_j[0], w_hi[0], x_lo, False, True).then_inc(S["proj_ps"], 1)
                    part(ps_j[1], w_hi[1], x_lo, False, True).then_inc(S["proj_ps"], 1)
                    part(ps_m[1], w_hi[2], x_hi, True, False)
                    part(ps_m[1], w_lo[2], x_hi, False, False)
                    part(ps_m[1], w_hi[2], x_lo, False, True).then_inc(S["proj_ps"], 1)
                if prv2:
                    pe.wait_ge(S["onehot"], u - 1)
                    pe.matmul(ps_m[0][:, POS0:POS0 + (GT + 1) * E0], before_bf[:, :], onehot[:, :, :],
                              start=True, stop=False, skip_group_check=True)
                    for t in range(GT):
                        mm = pe.matmul(ps_m[0][:, POS0 + (t + 1) * E0:POS0 + (GT + 1) * E0], ones_bf[:, :],
                                       onehot[:, t:t + 1, :].to_broadcast([P, GT - t, E0]),
                                       start=False, stop=(t == GT - 1), skip_group_check=True)
                    mm.then_inc(S["pos_ps"], 1)
            pipeline(pe, -1, GROUPS + 1, 2, (GROUPS - 4) // 2, step)

        @block.scalar
        def _(act):
            act.preload_act_table_set(LN_EXP)
            act.wait_ge(zero_first, 1)

            def copy(dst, src, s):
                act.activation(dst, src, ACT.Copy).then_inc(S[s], 1)

            def rsqrt(var, ln, out_, s_stat, s_ln, s_out, count):
                act.wait_ge(S[s_stat], count)
                act.activation(ln[:, :], var, ACT.Ln, bias=eps[:, 0:1]).then_inc(S[s_ln], 1)
                act.wait_ge(S[s_ln], count)
                act.activation(out_[:, :], ln[:, :], ACT.Exp, scale=-0.5).then_inc(S[s_out], 1)

            def normal(dst, src, r, nm, s_nm, s_out, count):
                act.wait_ge(S[s_nm], count)
                for t in range(GT):
                    ins = act.activation(dst(t), src(t), ACT.Identity, scale=r[:, t:t + 1], bias=nm[:, t:t + 1])
                ins.then_inc(S[s_out], 1)

            def vpad(u, c):
                act.wait_ge(S["k_out"], 4 * u + c + 1)
                if above_zero(4 * u + c - 1):
                    act.wait_ge(S["pv"], 4 * u + c - 1)
                copy(v_pad[c % 2][:, :, 0:4:3, :],
                     ps_j[c % 2][:, P:2 * P].rearrange("p (a r x) -> p a r x", a=H // 2, r=2), "v_pad")

            def step(u, half, g, n):
                o = 1 - g
                nxt, cur, prv, prv2 = (valid(n, k) for k in (1, 0, -1, -2))
                if nxt:
                    act.wait_ge(S["xt_ps"], u + 2)
                    if above_zero(u + 1):
                        act.wait_ge(S["h0_ps"], u + 1)
                    copy(xT_sb[0:FX, :], ps_m[0][0:FX, 0:P], "xt_sb")
                if cur:
                    vpad(u, 0)
                if prv2:
                    rsqrt(mv2[:, :, 1], lv2, r2, "st2", "ln2", "r2", u - 1)
                    act.activation(inv2[:, :], lv2[:, :], ACT.Exp, scale=-1.0).then_inc(S["inv2"], 1)
                if prv:
                    act.wait_ge(S["pv"], 4 * u)
                    if above_zero(u - 1):
                        act.wait_ge(S["var_ps"], u - 1)
                    if above_zero(u - 1):
                        act.wait_ge(S["t1"], u - 1)
                    act.activation(sq[:, :], ps_r[:, :], ACT.Square)
                    copy(cen[:, :], ps_r[:, :], "cen")
                if cur:
                    vpad(u, 1)
                if prv2:
                    if above_zero(u - 2):
                        act.wait_ge(S["x2T_ps"], u - 2)
                    if above_zero(u - 2):
                        act.wait_ge(S["xnn"], u - 2)
                    normal(lambda t: xn2[:, t, :], lambda t: tile(h, u - 2, t), r2, nm2, "nm2", "xn2", u - 1)
                if prv:
                    act.wait_ge(S["var_ps"], u)
                    act.activation(lvar[:, :], ps_g[:, :], ACT.Ln, bias=eps[:, 0:1]).then_inc(S["lvar"], 1)
                    act.wait_ge(S["lvar"], u)
                    act.activation(rstd[:, :], lvar[:, :], ACT.Exp, scale=-0.5).then_inc(S["rstd"], 1)
                if cur:
                    vpad(u, 2)
                if nxt:
                    rsqrt(mv1[:, :, 1], lv1, r1, "st1", "ln1", "r1", u + 2)
                if prv2:
                    act.wait_ge(S["x2T_ps"], u - 1)
                    copy(x2T[:, :], ps_m[0][:, :], "x2T_sb")
                    rsqrt(v3[:, :], lv3, r3, "v3", "ln3", "r3", u - 1)
                if prv:
                    act.preload_act_table_set("silu_and_others")
                if nxt:
                    if above_zero(u + 1):
                        act.wait_ge(S["xnT_ps"], u + 1)
                    normal(lambda t: xn[:, t, :], lambda t: tile(h, u + 1, t), r1, nm1, "nm1", "xn", u + 2)
                if prv:
                    act.wait_ge(S["t2"], u)
                    if above_zero(u - 1):
                        act.wait_ge(S["wo_ps"], u - 1)
                    act.activation(act_T[:, :], t2[:, :], ACT.Silu).then_inc(S["silu"], 1)
                if n == -1:
                    act.wait_ge(S["wv_ps"], 1)
                    copy(wv_T[:, :], ps_g[:, 0:P], "wv_sb")
                    act.wait_ge(S["wv_ps"], 2)
                    copy(wv[:, :], ps_g[:, P:2 * P], "wv_sb")
                    act.wait_ge(zero_done, 1)
                if cur:
                    vpad(u, 3)
                if nxt:
                    act.wait_ge(S["xnT_ps"], u + 2)
                    copy(x_hi[:, :], ps_m[1][:, :], "x_hi")
                    copy(xnT[o][:, :], ps_m[1][:, :], "xnT_sb")
                    for i, (dst, bank) in enumerate(((qT, ps_j[0]), (kT, ps_j[1]), (gT, ps_m[1]))):
                        act.wait_ge(S["proj_ps"], 3 * u + 4 + i)
                        if i == 0:
                            if above_zero(4 * u):
                                act.wait_ge(S["q_head"], 4 * u)
                            if above_zero(u):
                                act.wait_ge(S["q_in"], u)
                        copy(dst[o][:, :], bank[:, :], "proj_sb")
                if prv:
                    act.preload_act_table_set(LN_EXP)
            pipeline(act, -1, GROUPS + 1, 2, (GROUPS - 4) // 2, step)
            act.wait_ge(differences, 1)
            act.activation(expd[:, :, :], diff[:, :, :], ACT.Exp).then_inc(exps, 1)
            act.activation(e2[:, :], d2[:, :], ACT.Exp).then_inc(exps, 1)

        @block.vector
        def _(dve):
            dve.wait_ge(pos_done, 16)

            def stats(src, stat, mv, s_src, s_bn, s_out, count):
                dve.wait_ge(S[s_src], count)
                dve.sem_inc(passed, 1)
                for t in range(GT):
                    ins = dve.bn_stats(stat[:, t, :], src(t))
                ins.then_inc(S[s_bn], 1)
                dve.wait_ge(S[s_bn], count)
                dve.sem_inc(passed, 1)
                for t in range(GT):
                    ins = dve.bn_aggr(mv[:, t, :], stat[:, t, :])
                ins.then_inc(S[s_out], 1)

            def shift(nm, mv, r, s_r, s_out, count):
                dve.wait_ge(S[s_r], count)
                dve.scalar_tensor_tensor(nm[:, :], mv[:, :, 0], -1.0, r[:, :], ALU.mult,
                                         ALU.mult).then_inc(S[s_out], 1)

            def new_state(u, c):
                dve.wait_ge(S["st_ps"], 4 * u + c + 1)
                if above_zero(4 * u + c):
                    dve.wait_ge(S["state"], 4 * u + c)
                dve.tensor_tensor(s_new[:, :], ps_j[c % 2][:, 2 * P:3 * P], same_head[:, :],
                                  ALU.mult).then_inc(S["tmp"], 1)

            def chunk(u, g, c, prv=False):
                dve.wait_ge(S["kv_ps"], 4 * u + c + 1)
                if above_zero(4 * u + c - 1):
                    dve.wait_ge(S["st_ps"], 4 * u + c - 1)
                dve.tensor_tensor(k_out[c % 2][:, :], ps_j[c % 2][:, 0:P], k_decay[:, :],
                                  ALU.mult).then_inc(S["k_out"], 1)
                if c > 0:
                    new_state(u, c - 1)
                elif prv:
                    new_state(u - 1, GT - 1)
                if above_zero(4 * u + c - 1):
                    dve.wait_ge(S["pv"], 4 * u + c - 1)
                for half in (0, 1):
                    dve.wait_ge(S["score"], 8 * u + 2 * c + half + 1)
                    dve.tensor_tensor(prob[c % 2][:, 4 * half:4 * half + 4, :],
                                      ps_s[half][:, :].rearrange("p (a t) -> p a t", a=4),
                                      decay[:, 4 * half:4 * half + 4, :], ALU.mult).then_inc(S["prob"], 1)

            def state_up(u, g, c):
                if above_zero(4 * u + c):
                    dve.wait_ge(S["pv"], 4 * u + c)
                dve.wait_ge(S["tmp"], 4 * u + c + 1)
                if above_zero(4 * u + c):
                    dve.wait_ge(S["state"], 4 * u + c)
                dst = state[(c + 1) % 2]
                if g == 0 and c == 0:
                    dve.tensor_copy(dst[:, :], s_new[:, :]).then_inc(S["state"], 1)
                else:
                    dve.scalar_tensor_tensor(dst[:, :], state[c % 2][:, :], state_decay[:, 0:1], s_new[:, :],
                                             ALU.mult, ALU.add).then_inc(S["state"], 1)

            def step(u, half, g, n):
                o = 1 - g
                nxt, cur, prv, prv2 = (valid(n, k) for k in (1, 0, -1, -2))
                if n == 0:
                    dve.wait_ge(zero_done, 1)
                    dve.tensor_copy(before_bf[:, :], before[:, :])
                if prv2:
                    stats(lambda t: tile(h, u - 2, t), stat2, mv2, "h1", "bn2", "st2", u - 1)
                if cur:
                    chunk(u, g, 0, prv)
                if prv:
                    if not cur:
                        new_state(u - 1, 3)
                    state_up(u - 1, o, 3)
                if cur:
                    chunk(u, g, 1)
                if prv2:
                    shift(nm2, mv2, r2, "r2", "nm2", u - 1)
                    dve.wait_ge(S["inv2"], u - 1)
                    dve.tensor_tensor(v3[:, :], mv2[:, :, 1], inv2[:, :], ALU.mult).then_inc(S["v3"], 1)
                if cur:
                    state_up(u, g, 0)
                if nxt:
                    dve.wait_ge(S["h0_ps"], u + 2)
                    dve.tensor_tensor(h[:, bass.ds((u + 1) * GN, GN)], ps_m[1][:, :],
                                      pe_c[:, o * GT:(o + 1) * GT, :].rearrange("p t d -> p (t d)"),
                                      ALU.add).then_inc(S["h0"], 1)
                    stats(lambda t: tile(h, u + 1, t), stat1, mv1, "h0", "bn1", "st1", u + 2)
                if cur:
                    chunk(u, g, 2)
                    state_up(u, g, 1)
                if nxt:
                    shift(nm1, mv1, r1, "r1", "nm1", u + 2)
                if prv:
                    dve.wait_ge(S["rstd"], u)
                    dve.scalar_tensor_tensor(t1[:, :], cen[:, :], gn_w[:, 0:1], rstd[:, :],
                                             ALU.mult, ALU.mult).then_inc(S["t1"], 1)
                    dve.wait_ge(S["t1"], u)
                    dve.scalar_tensor_tensor(t2[:, :], t1[:, :], gn_b[:, 0:1], gT[o][:, :],
                                             ALU.add, ALU.add).then_inc(S["t2"], 1)
                if n == -1:
                    dve.wait_ge(const_done, 16 * N_CONST)
                    for hi, w in zip(w_hi, (wq, wk, wg)):
                        ins = dve.tensor_copy(hi[:, :], w[:, :])
                    ins.then_inc(S["w_parts"], 1)
                    dve.wait_ge(S["w_parts"], 1)
                    for lo, hi, w in zip(w_lo, w_hi, (wq, wk, wg)):
                        ins = dve.tensor_tensor(lo[:, :], w[:, :], hi[:, :].bitcast(F32), ALU.subtract)
                    ins.then_inc(S["w_parts"], 1)
                if cur:
                    chunk(u, g, 3)
                    state_up(u, g, 2)
                if prv2:
                    dve.wait_ge(S["logit_ps"], u - 1)
                    if above_zero(u - 2):
                        dve.wait_ge(S["kept"], u - 2)
                    dve.tensor_copy(lg[:, :, 0:E0],
                                    ps_m[0][:, 0:GT * LP].rearrange("p (t e) -> p t e", t=GT)[:, :, 0:E0]
                                    ).then_inc(S["logit"], 1)
                    dve.wait_ge(S["logit"], u - 1)
                    dve.sem_inc(passed, 1)
                    for tt in range(GT):
                        ins = dve.max(lg_top[:, tt, :], lg[:, tt, :])
                    ins.then_inc(S["top"], 1)
                    dve.wait_ge(S["top"], u - 1)
                    dve.sem_inc(passed, 1)
                    for tt in range(GT):
                        ins = dve.max_index(lg_at[:, tt, :], lg_top[:, tt, :], lg[:, tt, :])
                    ins.then_inc(S["top_i"], 1)
                    tiles = bass.ds((u - 2) * GT, GT)
                    dve.tensor_copy(logits[:, tiles, :], lg[:, :, :])
                    dve.tensor_copy(top[:, tiles, :], lg_top[:, :, :]).then_inc(S["kept"], 1)
                    dve.wait_ge(S["top_i"], u - 1)
                    dve.tensor_copy(choice[:, :], lg_at[:, :, 0]).then_inc(S["choice"], 1)
                    dve.wait_ge(S["choice"], u - 1)
                    dve.tensor_copy(m.choice[:, tiles], choice[:, :])
                    if above_zero(u - 2):
                        dve.wait_ge(S["pos_ps"], u - 2)
                    dve.tensor_tensor(onehot[:, 0:GT, :], choice[:, :].unsqueeze(2).to_broadcast([P, GT, E0]),
                                      expert_no[:, :].unsqueeze(1).to_broadcast([P, GT, E0]),
                                      ALU.is_equal).then_inc(S["onehot"], 1)
                if nxt:
                    dve.wait_ge(S["xnT_sb"], u + 2)
                    dve.tensor_tensor(x_lo[:, :], xnT[o][:, :], x_hi[:, :].bitcast(F32),
                                      ALU.subtract).then_inc(S["x_lo"], 1)
                if prv:
                    dve.wait_ge(S["wo_ps"], u)
                    hg = h[:, bass.ds((u - 1) * GN, GN)]
                    dve.tensor_tensor(hg, ps_g[:, :], hg, ALU.add).then_inc(S["h1"], 1)
                if prv2:
                    def before_it(first, last):
                        return ps_m[0][:, POS0 + first * E0:POS0 + last * E0]
                    dve.wait_ge(S["pos_ps"], u - 1)
                    if above_zero(u - 2):
                        dve.wait_ge(S["next_row"], u - 2)
                    dve.tensor_tensor(row_e[:, :, :], before_it(0, GT).rearrange("p (t e) -> p t e", t=GT),
                                      m.next_row[:, :].unsqueeze(1).to_broadcast([P, GT, E0]),
                                      ALU.add).then_inc(S["row_e"], 1)
                    dve.wait_ge(S["row_e"], u - 1)
                    dve.tensor_tensor(m.next_row[:, :], before_it(GT, GT + 1), m.next_row[:, :],
                                      ALU.add).then_inc(S["next_row"], 1)
                    dve.tensor_tensor(row_1[:, :, :], row_e[:, :, :], onehot[:, 0:GT, :],
                                      ALU.mult).then_inc(S["row_1"], 1)
                    dve.wait_ge(S["row_1"], u - 1)
                    dve.tensor_reduce(row_f[:, :], row_1[:, :, :], AXX, ALU.add).then_inc(S["row_f"], 1)
                    dve.wait_ge(S["row_f"], u - 1)
                    dve.tensor_copy(m.row[:, bass.ds((u - 2) * GT, GT)], row_f[:, :])
                    if above_zero(16 * GT * (half - 1)):
                        dve.wait_ge(m.s_scattered[g], 16 * GT * (half - 1))
                    dve.tensor_copy(row_i[g][:, :], row_f[:, :]).then_inc(S["slots"], 1)
            pipeline(dve, -1, GROUPS + 1, 2, (GROUPS - 4) // 2, step)

            dve.wait_ge(S["next_row"], GROUPS)
            dve.wait_ge(S["kept"], GROUPS)

            done = [0]

            def then(ins):
                done[0] += 1
                ins.then_inc(steps, 1)
                dve.wait_ge(steps, done[0])

            dve.tensor_copy(end_i[:, :], m.next_row[:, :]).then_inc(ended, 1)
            then(dve.tensor_tensor(n_f[:, :], m.next_row[:, :], region[:, :], ALU.subtract))
            then(dve.tensor_scalar(n_i[:, :], n_f[:, :], float(ET - 1), None, ALU.add))
            then(dve.tensor_scalar(n_tiles_i[:, :], n_i[:, :], ET.bit_length() - 1, None, ALU.logical_shift_right))
            then(dve.tensor_copy(n_tiles[:, :], n_tiles_i[:, :]))
            then(dve.tensor_tensor_scan(ends[:, :], m.ones[:, 0:E0], n_tiles[:, :], 0.0, ALU.mult, ALU.add))
            then(dve.tensor_tensor(starts[:, :], ends[:, :], n_tiles[:, :], ALU.subtract))
            dve.scalar_tensor_tensor(m.shift[:, :], starts[:, :], float(ET), region[:, :], ALU.mult, ALU.subtract)
            dve.tensor_scalar(skip[:, :], n_tiles[:, :], -float(ET), float(CAP), ALU.mult, ALU.add)
            then(dve.tensor_tensor(past[:, :, :], tile_no[:, :].unsqueeze(2).to_broadcast([P, NET, E0]),
                                   ends[:, :].unsqueeze(1).to_broadcast([P, NET, E0]), ALU.is_ge))
            dve.tensor_tensor(skips[:, :, :], past[:, :, :], skip[:, :].unsqueeze(1).to_broadcast([P, NET, E0]),
                              ALU.mult)
            then(dve.tensor_reduce(tile_f[:, :], past[:, :, 0:E0 - 1], AXX, ALU.add))
            dve.tensor_scalar(tile_off[:, :], tile_f[:, :], float(HID), None, ALU.mult)
            then(dve.tensor_reduce(row_s[:, :], skips[:, :, :], AXX, ALU.add))
            dve.tensor_copy(m.tile_e[:, :], tile_off[:, :])
            then(dve.scalar_tensor_tensor(tile_row_f[:, :], tile_no[:, :], float(ET), row_s[:, :], ALU.mult, ALU.add))
            dve.tensor_copy(m.tile_row[:, :], tile_row_f[:, :])
            dve.tensor_tensor(d2[:, :], m.top[:, :, 1], m.top[:, :, 0], ALU.subtract)
            dve.tensor_tensor(diff[:, :, :], m.logits[:, :, 0:E0],
                              m.top[:, :, 0:1].to_broadcast([P, TILES, E0]), ALU.subtract).then_inc(differences, 1)
            dve.wait_ge(exps, 2)
            then(dve.tensor_reduce(total[:, :], expd[:, :, :], AXX, ALU.add))
            then(dve.scalar_tensor_tensor(den[:, :], total[:, :], GATE_EPS, e2[:, :], ALU.mult, ALU.add))
            then(dve.tensor_scalar(den[:, :], den[:, :], 1.0, None, ALU.add))
            then(dve.reciprocal(m.gate[:, :], den[:, :]))


def phase2(nc, ctx, ph, m, t, cst, out):
    def sb(name, shape, dt=F32):
        return ph.enter_context(nc.sbuf_tensor(name, shape, dt))

    def psum(name, shape, dt=F32):
        return ph.enter_context(nc.psum_tensor(name, shape, dt))

    def sem(name):
        return ctx.enter_context(nc.semaphore(name))

    RS = ET // P
    xe = [sb(f"xe{i}", [P, RS, P]) for i in (0, 1)]
    x_hi, x_lo = ([sb(f"{n}{i}", [P, ET], F32R) for i in (0, 1)] for n in ("x_hi", "x_lo"))
    w_hi, w_lo = ([sb(f"{n}{i}", [P, HID], F32R) for i in (0, 1)] for n in ("w_hi", "w_lo"))
    hid = [sb(f"hid{i}", [P, HB, ET]) for i in (0, 1)]
    y_sb = [sb(f"y_sb{i}", [P, RS, P]) for i in (0, 1)]
    ps_t = [psum(f"ps_t{i}", [P, 512]) for i in (0, 1)]
    ps_h = [psum(f"ps_h{i}", [P, HB, ET]) for i in (0, 1)]
    ps_y = [psum(f"ps_y{i}", [P, 512]) for i in (0, 1)]
    passed = m.passed
    xe_ld = [sem(f"p2_xe_ld{i}") for i in (0, 1)]
    y_st = [sem(f"p2_y_st{i}") for i in (0, 1)]
    names = "xT_ps x_hi x_lo w_hi w_lo h_ps hid y_ps y_sb shift_e slot_f".split()
    S = {n: sem("p2_" + n) for n in names}
    ys_t = m.ys_dram.rearrange("(a p) d -> p a d", p=P)
    shift_e = sb("shift_e", [P, TILES])
    PAIRS = (NET - 4) // 2

    def valid(n, k):
        return n is None or 0 <= n + k < NET

    def offset(eng, j):
        return eng.value_load(m.tile_e[0:1, bass.ds(j, 1)], min_val=0, max_val=(E0 - 1) * HID)

    with nc.Block() as block:
        @block.gpsimd
        def _(pool):
            for e in range(E0):
                if e > 0:
                    pool.wait_ge(S["slot_f"], e)
                pool.tensor_scalar(shift_e[:, :], m.choice[:, :], float(e), m.shift[:, e:e + 1],
                                   ALU.is_equal, ALU.mult).then_inc(S["shift_e"], 1)
                pool.wait_ge(S["shift_e"], e + 1)
                pool.tensor_tensor(m.row[:, :], m.row[:, :], shift_e[:, :], ALU.add).then_inc(S["slot_f"], 1)
            pool.wait_ge(S["slot_f"], E0)
            pool.tensor_copy(m.slots[:, :], m.row[:, :])

        @block.sync
        def _(sp):
            for i in (0, 1):
                sp.wait_ge(m.s_scattered[i], 16 * TILES // 2)
            sp.wait_ge(m.s_padded, 16 * E0)
            sp.wait_ge(m.s_experts, 16 * N_EXPERT)

            def rows(j):
                row = sp.value_load(m.tile_row[0:1, bass.ds(j, 1)], min_val=0, max_val=ROWS - ET)
                return m.xs_dram[bass.ds(row, ET), :].rearrange("(a p) d -> p a d", p=P)

            for n in (0, 1):
                sp.dma_start(xe[n][:, :, :], rows(n)).then_inc(xe_ld[n], 16)

            def step(j, half, g, n):
                if valid(n, 0) and valid(n, 2):
                    src = rows(j + 2)
                    sp.wait_ge(S["xT_ps"], j + 1)
                    sp.dma_start(xe[g][:, :, :], src).then_inc(xe_ld[g], 16)
                if valid(n, -2):
                    sp.wait_ge(S["y_sb"], j - 1)
                    sp.dma_start(ys_t[:, bass.ds(RS * (j - 2), RS), :], y_sb[g][:, :, :]).then_inc(y_st[g], 16)
            pipeline(sp, -1, NET + 1, 2, PAIRS, step)
            for i in (0, 1):
                sp.wait_ge(y_st[i], 16 * ((NET + 1 - i) // 2))

        @block.tensor
        def _(pe):
            def step(j, half, g, n):
                o = 1 - g
                if valid(n, -1):
                    off = offset(pe, j - 1)
                if valid(n, 1):
                    pe.wait_ge(xe_ld[o], 16 * (half + g + 1))
                    if above_zero(j):
                        pe.wait_ge(S["x_lo"], j)
                    for s in range(RS):
                        mm = pe.transpose(ps_t[o][:, s * P:(s + 1) * P], xe[o][:, s, :], m.ident[:, :])
                    mm.then_inc(S["xT_ps"], 1)
                if valid(n, 0):
                    pe.wait_ge(S["x_lo"], j + 1)
                    pe.wait_ge(S["w_lo"], j + 1)
                    if above_zero(j - 1):
                        pe.wait_ge(S["hid"], j - 1)
                    for k in range(HB):
                        ks = slice(k * P, (k + 1) * P)
                        pe.matmul(ps_h[g][:, k, :], w_hi[g][:, ks], x_hi[g][:, :], start=True, stop=False)
                        pe.matmul(ps_h[g][:, k, :], w_hi[g][:, ks], x_lo[g][:, :], start=False, stop=False)
                        mm = pe.matmul(ps_h[g][:, k, :], w_lo[g][:, ks], x_hi[g][:, :], start=False, stop=True)
                    mm.then_inc(S["h_ps"], 1)
                if valid(n, -1):
                    pe.wait_ge(S["hid"], j)
                    if above_zero(j - 2):
                        pe.wait_ge(S["y_sb"], j - 2)
                    for s in range(RS):
                        for k in range(HB):
                            mm = pe.matmul(ps_y[o][:, s * P:(s + 1) * P], hid[o][:, k, s * P:(s + 1) * P],
                                           m.w2[:, bass.ds(off + k * P, P)], start=(k == 0), stop=(k == HB - 1))
                    mm.then_inc(S["y_ps"], 1)
            pipeline(pe, -1, NET, 2, PAIRS, step)

        @block.scalar
        def _(act):
            act.preload_act_table_set("gelu_and_others")

            def step(j, half, g, n):
                o = 1 - g
                if valid(n, 1):
                    act.wait_ge(S["xT_ps"], j + 2)
                    if above_zero(j):
                        act.wait_ge(S["h_ps"], j)
                    act.activation(x_hi[o][:, :], ps_t[o][:, 0:ET], ACT.Copy).then_inc(S["x_hi"], 1)
                if valid(n, 0):
                    act.wait_ge(S["h_ps"], j + 1)
                    if above_zero(j - 1):
                        act.wait_ge(S["y_ps"], j - 1)
                    act.activation(hid[g][:, :, :], ps_h[g][:, :, :], ACT.Gelu).then_inc(S["hid"], 1)
            pipeline(act, -1, NET, 2, PAIRS, step)

        @block.vector
        def _(dve):
            def step(j, half, g, n):
                o = 1 - g
                if valid(n, 1):
                    if above_zero(j):
                        dve.wait_ge(S["h_ps"], j)
                    off = offset(dve, j + 1)
                    dve.tensor_copy(w_hi[o][:, :], m.w1[:, bass.ds(off, HID)]).then_inc(S["w_hi"], 1)
                    dve.wait_ge(S["x_hi"], j + 2)
                    dve.tensor_tensor(x_lo[o][:, :], ps_t[o][:, 0:ET], x_hi[o][:, :].bitcast(F32),
                                      ALU.subtract).then_inc(S["x_lo"], 1)
                    dve.wait_ge(S["w_hi"], j + 2)
                    dve.tensor_tensor(w_lo[o][:, :], m.w1[:, bass.ds(off, HID)], w_hi[o][:, :].bitcast(F32),
                                      ALU.subtract).then_inc(S["w_lo"], 1)
                if valid(n, -1):
                    dve.wait_ge(S["y_ps"], j)
                    if above_zero(16 * (half + g - 1)):
                        dve.wait_ge(y_st[o], 16 * (half + g - 1))
                    dve.tensor_copy(y_sb[o][:, :, :], ps_y[o][:, 0:ET].rearrange("p (s d) -> p s d", s=RS)
                                    ).then_inc(S["y_sb"], 1)
            dve.wait_ge(m.s_experts, 16 * N_EXPERT)
            pipeline(dve, -1, NET, 2, PAIRS, step)


def phase3(nc, ctx, ph, m, t, cst, out):
    h, ident, ones, eps = m.h, m.ident, m.ones, m.eps
    back = ph.enter_context(nc.sbuf_tensor("back", [P, TILES * P], F32))

    def sb(name, shape, dt=F32):
        return ph.enter_context(nc.sbuf_tensor("p3_" + name, shape, dt))

    def psum(name, shape, dt=F32):
        return ph.enter_context(nc.psum_tensor("p3_" + name, shape, dt))

    def sem(name):
        return ctx.enter_context(nc.semaphore(name))

    w_ld = sb("w_ld", [P, 3, P])
    w_T = sb("w_T", [P, 3, P])
    b_q = sb("b_q", [P, 1])
    b_k = sb("b_k", [P, 1])
    b_v = sb("b_v", [P, P])
    w_r = sb("w_r", [P, LP])
    b_r = sb("b_r", [P, E1])
    stat = sb("stat", [P, TPB, 6])
    mv = sb("mv", [P, TPB, 2])
    lv = sb("lv", [P, TPB])
    rs = sb("rs", [P, TPB])
    nm = sb("nm", [P, TPB])
    stat_f = sb("stat_f", [P, TPB, 6])
    mv_f = sb("mv_f", [P, TPB, 2])
    lv_f = sb("lv_f", [P, TPB])
    rs_f = sb("rs_f", [P, TPB])
    nm_f = sb("nm_f", [P, TPB])
    xf = sb("xf", [P, TPB, P])
    xn = sb("xn", [P, TPB, P])
    xnT = sb("xnT", [P, SEQ])
    q_hi, q_lo, k_hi, k_lo = ([sb(f"{n}{i}", [P, SEQ], F32R) for i in (0, 1)]
                              for n in ("q_hi", "q_lo", "k_hi", "k_lo"))
    val = [sb(f"val{i}", [P, TPB, P]) for i in (0, 1)]
    top_s = sb("top_s", [P, TPB])
    bias_s = sb("bias_s", [P, TPB])
    sum_s = sb("sum_s", [P, TPB])
    inv_s = sb("inv_s", [P, TPB])
    prob = [sb(f"prob{i}", [P, SEQ]) for i in (0, 1)]
    val_n = [sb(f"val_n{i}", [P, P]) for i in (0, 1)]
    h3c = sb("h3c", [P, TPB, P])
    xfT = sb("xfT", [P, SEQ])
    xf_sum = sb("xf_sum", [P, 2])
    mean1 = sb("mean1", [P, 1])
    mean = sb("mean", [P, P])
    lg = sb("lg", [P, E1])
    lg_top = sb("lg_top", [P, 1])
    ex = sb("ex", [P, E1])
    ex_sum = sb("ex_sum", [P, 1])
    ex_top = sb("ex_top", [P, 8])
    ex_at = sb("ex_at", [P, 8], U32)
    gate = [sb(f"gate{i}", [P, 1]) for i in (0, 1)]
    we = [sb(f"we{i}", [P, P]) for i in (0, 1)]
    be = [sb(f"be{i}", [P, P]) for i in (0, 1)]
    y1 = sb("y1", [P, SEQ])
    o_sb = [sb(f"o_sb{i}", [P, TPB, P]) for i in (0, 1)]

    ps_s = [psum(f"ps_s{i}", [P, SEQ]) for i in (0, 1)]
    ps_o = psum("ps_o", [P, SEQ])
    ps_f = [psum(f"ps_f{i}", [P, 512]) for i in (0, 1)]

    const_done, zero_done, passed = sem("p3_const_ld"), sem("p3_zeroed"), m.passed
    gathered_0 = [sem(f"p3_gathered_0_{q}") for q in (0, 1)]
    gathered = [sem(f"p3_gathered{i}") for i in (0, 1)]
    we_ld = [sem(f"p3_we_ld{i}") for i in (0, 1)]
    o_st = [sem(f"p3_o_st{i}") for i in (0, 1)]
    names = ("wT_ps wT_sb h2_0 gated h2 bn st ln rs nm xc xn xT_ps xT_sb q_ps q_hi q_lo k_ps k_hi k_lo v_ps v_sb score top "
             "bias exp inv val_n av h3 bn_f st_f ln_f rs_f nm_f xf hT_ps hT_sb mean1 mean r_ps lg lg_top ex ex_top ex_at gate "
             "y_ps y1 out").split()
    S = {n: sem("p3_did_" + n) for n in names}
    N_C4 = 9
    out_t = out.rearrange("b (c p) d -> b p c d", p=P)
    PAIRS = (B - 4) // 2

    def valid(n, k):
        return n is None or 0 <= n + k < B

    def tile(buf, u, tt):
        return buf[:, bass.ds(u * SEQ + tt * P, P)]

    with nc.Block() as block:
        @block.sync
        def _(sp):
            sp.dma_start(w_ld[:, 0, :], t["L1_attn_Wq"]).then_inc(const_done, 16)
            sp.dma_start(w_ld[:, 1, :], t["L1_attn_Wk"]).then_inc(const_done, 16)
            sp.dma_start(w_ld[:, 2, :], t["L1_attn_Wv"]).then_inc(const_done, 16)
            sp.dma_start(b_q[:, :], t["L1_attn_bq"].unsqueeze(1)).then_inc(const_done, 16)
            sp.dma_start(b_k[:, :], t["L1_attn_bk"].unsqueeze(1)).then_inc(const_done, 16)
            sp.dma_start(b_v[:, :], t["L1_attn_bv"].partition_broadcast(P)).then_inc(const_done, 16)
            sp.dma_start(b_r[:, :], t["L1_ffn_bg"].partition_broadcast(P)).then_inc(const_done, 16)
            sp.wait_ge(zero_done, 1)
            sp.dma_start(w_r[:, 0:E1], t["L1_ffn_Wg"]).then_inc(const_done, 16)

            def step(u, half, g, n):
                o = 1 - g
                if valid(n, -1):
                    if above_zero(2 * u - 4):
                        sp.wait_ge(S["out"], 2 * u - 4)
                    sp.sem_inc(passed, 1)
                    sp.wait_ge(S["ex_at"], u)
                    sp.sem_inc(passed, 1)
                    at = sp.value_load(ex_at[0:1, 0:1], min_val=0, max_val=E1 - 1)
                    sp.dma_start(we[o][:, :], t["L1_ffn_We"][bass.ds(at, 1), :, :].rearrange("a d o -> (a d) o")
                                 ).then_inc(we_ld[o], 16)
                    sp.dma_start(be[o][:, :], t["L1_ffn_be"][bass.ds(at, 1), :].rearrange("a o -> (a o)")
                                 .partition_broadcast(P)).then_inc(we_ld[o], 16)
                    for hf in (0, 1):
                        sp.wait_ge(S["out"], 2 * (u - 1) + hf + 1)
                        sp.dma_start(out_t[bass.ds(u - 1, 1), :, 4 * hf:4 * hf + 4, :]
                                     .rearrange("b p c d -> (b p) c d"),
                                     o_sb[o][:, 4 * hf:4 * hf + 4, :]).then_inc(o_st[o], 16)
            pipeline(sp, -1, B, 2, PAIRS, step)
            for i in (0, 1):
                sp.wait_ge(o_st[i], 32 * (B // 2))

        @block.gpsimd
        def _(pool):
            pool.memset(w_r[:, :], 0.0).then_inc(zero_done, 1)

            def gather(u):
                if u >= 3:
                    pool.wait_ge(gathered[u % 2], 16 * TPB * (u // 2 - 1 + u % 2))
                for q in range(TPB):
                    i = u * TPB + q
                    done = gathered_0[q // 4] if u == 0 else gathered[u % 2]
                    pool.indirect_dma_start(
                        out=back[:, i * P:(i + 1) * P], out_offset=None, in_=m.ys_dram,
                        in_offset=bass.IndirectOffsetOnAxis(ap=m.slots[:, i:i + 1], axis=0)
                    ).then_inc(done, 16)

            def add_experts(u):
                pool.wait_ge(gathered[u % 2], 16 * TPB * (u // 2 + u % 2))
                cols = slice(u * SEQ, (u + 1) * SEQ)
                rows = back[:, cols].rearrange("p (a d) -> p a d", a=TPB)
                pool.tensor_tensor(rows, rows,
                                   m.gate[:, u * TPB:(u + 1) * TPB].unsqueeze(2).to_broadcast([P, TPB, P]),
                                   ALU.mult).then_inc(S["gated"], 1)
                pool.wait_ge(S["gated"], u)
                pool.tensor_tensor(h[:, cols], back[:, cols], h[:, cols], ALU.add).then_inc(S["h2"], 1)

            def normal(u):
                pool.wait_ge(S["rs"], u + 1)
                pool.wait_ge(S["xT_ps"], 2 * u)
                halves = (slice(0, 4), slice(4, 8))
                h_u = h[:, u * SEQ:(u + 1) * SEQ].rearrange("p (a d) -> p a d", a=TPB)
                for hf in halves:
                    pool.tensor_tensor(xn[:, hf, :], h_u[:, hf, :], mv[:, hf, 0:1].to_broadcast([P, 4, P]),
                                       ALU.subtract).then_inc(S["xc"], 1)
                for n, hf in enumerate(halves):
                    pool.wait_ge(S["xc"], 2 * (u - 1) + n + 1)
                    pool.tensor_tensor(xn[:, hf, :], xn[:, hf, :], rs[:, hf].unsqueeze(2).to_broadcast([P, 4, P]),
                                       ALU.mult).then_inc(S["xn"], 1)

            gather(0)
            gather(1)
            for u in range(2, B):
                gather(u)
                add_experts(u - 1)
                normal(u - 1)
            add_experts(B - 1)
            normal(B - 1)

        @block.tensor
        def _(pe):
            pe.wait_ge(const_done, 16 * (N_C4 - 1))
            for i in range(3):
                mm = pe.transpose(ps_f[0][:, i * P:(i + 1) * P], w_ld[:, i, :], ident[:, :])
            mm.then_inc(S["wT_ps"], 1)
            pe.wait_ge(S["wT_sb"], 1)

            def project(i, s, bank_free, u):
                for hf in (0, 1):
                    pe.wait_ge(S[bank_free], 2 * (u + 1) + hf + 1)
                    pe.matmul(ps_f[hf][:, :], w_T[:, i, :], xnT[:, hf * 512:(hf + 1) * 512],
                              start=True, stop=True).then_inc(S[s], 1)

            def step(u, half, g, n):
                o = 1 - g
                nxt, cur, prv = (valid(n, k) for k in (1, 0, -1))

                def scores(kt):
                    if kt == 0:
                        pe.wait_ge(S["q_lo"], 2 * u + 2)
                        pe.wait_ge(S["k_lo"], 2 * u + 2)
                    if above_zero(8 * u + kt - 1):
                        pe.wait_ge(S["exp"], 8 * u + kt - 1)
                    for hf in (0, 1):
                        qs, ks = slice(hf * 512, (hf + 1) * 512), slice(kt * P, (kt + 1) * P)
                        pe.matmul(ps_s[kt % 2][:, qs], k_hi[g][:, ks], q_hi[g][:, qs], start=True, stop=False)
                        pe.matmul(ps_s[kt % 2][:, qs], k_hi[g][:, ks], q_lo[g][:, qs], start=False, stop=False)
                        mm = pe.matmul(ps_s[kt % 2][:, qs], k_lo[g][:, ks], q_hi[g][:, qs], start=False, stop=True)
                    mm.then_inc(S["score"], 1)

                def av(uu, kt):
                    if kt == 0:
                        if above_zero(uu):
                            pe.wait_ge(S["h3"], uu)
                    pe.wait_ge(S["val_n"], 8 * uu + kt + 1)
                    for q in range(TPB):
                        mm = pe.matmul(ps_o[:, q * P:(q + 1) * P], prob[kt % 2][:, q * P:(q + 1) * P],
                                       val_n[kt % 2][:, :], start=(kt == 0 and q % 4 == 0),
                                       stop=(kt == TPB - 1), skip_group_check=True)
                    mm.then_inc(S["av"], 1)

                if cur:
                    scores(0)
                if prv:
                    av(u - 1, 7)
                if cur:
                    scores(1)
                    scores(2)
                    av(u, 0)
                    scores(3)
                    av(u, 1)
                    scores(4)
                    av(u, 2)
                    scores(5)
                if prv:
                    if cur:
                        pe.wait_ge(S["v_sb"], 2 * u + 2)
                    if above_zero(2 * u - 2):
                        pe.wait_ge(S["y1"], 2 * u - 2)
                    for hf in (0, 1):
                        pe.wait_ge(S["xf"], 2 * (u - 1) + hf + 1)
                        for q in range(4):
                            mm = pe.transpose(ps_f[hf][:, q * P:(q + 1) * P], xf[:, 4 * hf + q, :], ident[:, :])
                        mm.then_inc(S["hT_ps"], 1)
                if cur:
                    av(u, 3)
                    scores(6)
                    av(u, 4)
                if prv:
                    pe.wait_ge(S["mean"], u)
                    pe.matmul(ps_f[0][:, 0:LP], mean[:, :], w_r[:, :], start=True, stop=True).then_inc(S["r_ps"], 1)
                if cur:
                    scores(7)
                if nxt:
                    if prv:
                        pe.wait_ge(S["lg"], u)
                    elif cur:
                        pe.wait_ge(S["v_sb"], 2 * u + 2)
                    for hf in (0, 1):
                        pe.wait_ge(S["xn"], 2 * (u + 1) + hf + 1)
                        for q in range(4):
                            mm = pe.transpose(ps_f[hf][:, q * P:(q + 1) * P], xn[:, 4 * hf + q, :], ident[:, :])
                        mm.then_inc(S["xT_ps"], 1)
                if nxt:
                    project(0, "q_ps", "xT_sb", u)
                if cur:
                    av(u, 5)
                if nxt:
                    project(1, "k_ps", "q_lo", u)
                if cur:
                    av(u, 6)
                if nxt:
                    for hf in (0, 1):
                        pe.wait_ge(S["k_lo"], 2 * (u + 1) + hf + 1)
                        for q in range(4):
                            mm = pe.matmul(ps_f[hf][:, q * P:(q + 1) * P], xnT[:, (4 * hf + q) * P:(4 * hf + q + 1) * P],
                                           w_T[:, 2, :], start=True, stop=True)
                        mm.then_inc(S["v_ps"], 1)
                if prv:
                    pe.wait_ge(we_ld[o], 32 * (half + g))
                    for hf in (0, 1):
                        if nxt:
                            pe.wait_ge(S["v_sb"], 2 * (u + 1) + hf + 1)
                        for q in range(4):
                            mm = pe.matmul(ps_f[hf][:, q * P:(q + 1) * P],
                                           xfT[:, (4 * hf + q) * P:(4 * hf + q + 1) * P], we[o][:, :],
                                           start=True, stop=True)
                        mm.then_inc(S["y_ps"], 1)
            pipeline(pe, -1, B, 2, PAIRS, step)

        @block.scalar
        def _(act):
            act.preload_act_table_set(LN_EXP)
            act.wait_ge(S["wT_ps"], 1)
            act.activation(w_T[:, :, :], ps_f[0][:, 0:3 * P].rearrange("p (a d) -> p a d", a=3),
                           ACT.Copy).then_inc(S["wT_sb"], 1)

            def from_f(dst, filled, emptied, u, func=ACT.Copy, **kw):
                for hf in (0, 1):
                    act.wait_ge(S[filled], 2 * (u + 1) + hf + 1)
                    act.activation(dst[:, hf * 512:(hf + 1) * 512], ps_f[hf][:, :], func,
                                   **kw).then_inc(S[emptied], 1)

            def step(u, half, g, n):
                o = 1 - g
                nxt, cur, prv = (valid(n, k) for k in (1, 0, -1))

                def exp(kt):
                    if above_zero(8 * u + kt - 1):
                        act.wait_ge(S["av"], 8 * u + kt - 1)
                    act.wait_ge(S["bias"], 8 * u + kt + 1)
                    act.activation(prob[kt % 2][:, :], ps_s[kt % 2][:, :], ACT.Exp, scale=SCALE1,
                                   bias=bias_s[:, kt:kt + 1], accum_out=sum_s[:, kt:kt + 1]).then_inc(S["exp"], 1)

                if cur:
                    exp(0)
                    exp(1)
                    exp(2)
                if prv:
                    act.wait_ge(S["st_f"], u)
                    act.activation(lv_f[:, :], mv_f[:, :, 1], ACT.Ln, bias=eps[:, 0:1]).then_inc(S["ln_f"], 1)
                    act.wait_ge(S["ln_f"], u)
                    act.activation(rs_f[:, :], lv_f[:, :], ACT.Exp, scale=-0.5).then_inc(S["rs_f"], 1)
                if cur:
                    exp(3)
                if prv:
                    act.wait_ge(S["nm_f"], u)
                    if above_zero(2 * u - 2):
                        act.wait_ge(S["hT_ps"], 2 * u - 2)
                    for hf in (0, 1):
                        for q in range(4 * hf, 4 * hf + 4):
                            ins = act.activation(xf[:, q, :], h3c[:, q, :], ACT.Identity, scale=rs_f[:, q:q + 1],
                                                 bias=nm_f[:, q:q + 1])
                        ins.then_inc(S["xf"], 1)
                if cur:
                    exp(4)
                if nxt:
                    act.wait_ge(S["st"], u + 2)
                    act.activation(lv[:, :], mv[:, :, 1], ACT.Ln, bias=eps[:, 0:1]).then_inc(S["ln"], 1)
                    act.wait_ge(S["ln"], u + 2)
                    act.activation(rs[:, :], lv[:, :], ACT.Exp, scale=-0.5).then_inc(S["rs"], 1)
                if prv:
                    if above_zero(2 * u - 2):
                        act.wait_ge(S["y_ps"], 2 * u - 2)
                    if above_zero(u - 1):
                        act.wait_ge(S["mean1"], u - 1)
                    for hf in (0, 1):
                        act.wait_ge(S["hT_ps"], 2 * (u - 1) + hf + 1)
                        ins = act.activation(xfT[:, hf * 512:(hf + 1) * 512], ps_f[hf][:, :], ACT.Identity,
                                             accum_out=xf_sum[:, hf:hf + 1])
                    ins.then_inc(S["hT_sb"], 1)
                if cur:
                    exp(5)
                if n == -1:
                    act.wait_ge(S["nm"], u + 2)
                    if above_zero(2 * u + 2):
                        act.wait_ge(S["xT_ps"], 2 * u + 2)
                    for hf in (0, 1):
                        for q in range(4 * hf, 4 * hf + 4):
                            ins = act.activation(xn[:, q, :], tile(h, u + 1, q), ACT.Identity, scale=rs[:, q:q + 1],
                                                 bias=nm[:, q:q + 1])
                        ins.then_inc(S["xn"], 1)
                if cur:
                    exp(6)
                if prv:
                    act.wait_ge(S["lg_top"], u)
                    act.activation(ex[:, :], lg[:, :], ACT.Exp, bias=lg_top[:, 0:1],
                                   accum_out=ex_sum[:, 0:1]).then_inc(S["ex"], 1)
                if nxt:
                    from_f(xnT, "xT_ps", "xT_sb", u)
                if nxt:
                    from_f(q_hi[o], "q_ps", "q_hi", u, ACT.Identity, bias=b_q[:, 0:1])
                if cur:
                    exp(7)
                if nxt:
                    from_f(k_hi[o], "k_ps", "k_hi", u, ACT.Identity, bias=b_k[:, 0:1])
            pipeline(act, -1, B, 2, PAIRS, step)

        @block.vector
        def _(dve):
            dve.wait_ge(const_done, 16 * (N_C4 - 1))

            def step(u, half, g, n):
                o = 1 - g
                nxt, cur, prv = (valid(n, k) for k in (1, 0, -1))

                def tops(kt):
                    dve.wait_ge(S["score"], 8 * u + kt + 1)
                    if above_zero(8 * u + kt - 7):
                        dve.wait_ge(S["exp"], 8 * u + kt - 7)
                    dve.tensor_reduce(top_s[:, kt:kt + 1], ps_s[kt % 2][:, :], AXX, ALU.max).then_inc(S["top"], 1)
                    dve.wait_ge(S["top"], 8 * u + kt + 1)
                    dve.tensor_scalar(bias_s[:, kt:kt + 1], top_s[:, kt:kt + 1], -SCALE1, None,
                                      ALU.mult).then_inc(S["bias"], 1)

                def low_part(lo, hi, bias, did_hi, did_lo, u):
                    for hf in (0, 1):
                        cols = slice(hf * 512, (hf + 1) * 512)
                        dve.wait_ge(S[did_hi], 2 * (u + 1) + hf + 1)
                        dve.scalar_tensor_tensor(lo[:, cols], ps_f[hf][:, :], bias[:, 0:1], hi[:, cols].bitcast(F32),
                                                 ALU.add, ALU.subtract).then_inc(S[did_lo], 1)

                def values(kt):
                    dve.wait_ge(S["exp"], 8 * u + kt + 1)
                    dve.reciprocal(inv_s[:, kt:kt + 1], sum_s[:, kt:kt + 1]).then_inc(S["inv"], 1)
                    dve.wait_ge(S["inv"], 8 * u + kt + 1)
                    if above_zero(8 * u + kt - 1):
                        dve.wait_ge(S["av"], 8 * u + kt - 1)
                    dve.tensor_scalar(val_n[kt % 2][:, :], val[g][:, kt, :], inv_s[:, kt:kt + 1], None,
                                      ALU.mult).then_inc(S["val_n"], 1)

                if cur:
                    tops(0)
                if prv:
                    dve.wait_ge(S["av"], 8 * u)
                    if above_zero(2 * u - 2):
                        dve.wait_ge(S["out"], 2 * u - 2)
                    for hf in (0, 1):
                        ins = dve.tensor_tensor(h3c[:, 4 * hf:4 * hf + 4, :].rearrange("p a d -> p (a d)"),
                                                ps_o[:, hf * 512:(hf + 1) * 512],
                                                h[:, bass.ds((u - 1) * SEQ + hf * 512, 512)], ALU.add)
                    ins.then_inc(S["h3"], 1)
                if cur:
                    tops(1)
                    values(0)
                if prv:
                    dve.wait_ge(S["h3"], u)
                    dve.sem_inc(passed, 1)
                    for q in range(TPB):
                        ins = dve.bn_stats(stat_f[:, q, :], h3c[:, q, :])
                    ins.then_inc(S["bn_f"], 1)
                if cur:
                    tops(2)
                    values(1)
                if prv:
                    dve.wait_ge(S["bn_f"], u)
                    dve.sem_inc(passed, 1)
                    for q in range(TPB):
                        ins = dve.bn_aggr(mv_f[:, q, :], stat_f[:, q, :])
                    ins.then_inc(S["st_f"], 1)
                if n == -1:
                    for q in range(TPB):
                        dve.wait_ge(gathered_0[q // 4], 16 * 4)
                        ins = dve.scalar_tensor_tensor(tile(h, 0, q), tile(back, 0, q), m.gate[:, q:q + 1],
                                                       tile(h, 0, q), ALU.mult, ALU.add)
                    ins.then_inc(S["h2_0"], 1)
                if cur:
                    tops(3)
                if prv:
                    dve.wait_ge(S["rs_f"], u)
                    dve.scalar_tensor_tensor(nm_f[:, :], mv_f[:, :, 0], -1.0, rs_f[:, :], ALU.mult,
                                             ALU.mult).then_inc(S["nm_f"], 1)
                if cur:
                    values(2)
                if nxt:
                    if n == -1:
                        dve.wait_ge(S["h2_0"], 1)
                    else:
                        dve.wait_ge(S["h2"], u + 1)
                    dve.sem_inc(passed, 1)
                    for q in range(TPB):
                        ins = dve.bn_stats(stat[:, q, :], tile(h, u + 1, q))
                    ins.then_inc(S["bn"], 1)
                if cur:
                    tops(4)
                    values(3)
                if nxt:
                    dve.wait_ge(S["bn"], u + 2)
                    if above_zero(2 * u + 2):
                        dve.wait_ge(S["xn"], 2 * u + 2)
                    dve.sem_inc(passed, 1)
                    for q in range(TPB):
                        ins = dve.bn_aggr(mv[:, q, :], stat[:, q, :])
                    ins.then_inc(S["st"], 1)
                if cur:
                    tops(5)
                if n == -1:
                    dve.wait_ge(S["rs"], u + 2)
                    dve.scalar_tensor_tensor(nm[:, :], mv[:, :, 0], -1.0, rs[:, :], ALU.mult,
                                             ALU.mult).then_inc(S["nm"], 1)
                if cur:
                    values(4)
                if prv:
                    dve.wait_ge(S["hT_sb"], u)
                    dve.tensor_tensor(mean1[:, :], xf_sum[:, 0:1], xf_sum[:, 1:2], ALU.add).then_inc(S["mean1"], 1)
                    dve.wait_ge(S["mean1"], u)
                    dve.tensor_scalar(mean[:, :], ones[:, :], mean1[:, 0:1], 1.0 / SEQ, ALU.mult,
                                      ALU.mult).then_inc(S["mean"], 1)
                if cur:
                    tops(6)
                if prv:
                    dve.wait_ge(S["r_ps"], u)
                    dve.tensor_tensor(lg[:, :], ps_f[0][:, 0:E1], b_r[:, :], ALU.add).then_inc(S["lg"], 1)
                    dve.wait_ge(S["lg"], u)
                    dve.tensor_reduce(lg_top[:, :], lg[:, :], AXX, ALU.max, negate=True).then_inc(S["lg_top"], 1)
                if cur:
                    values(5)
                    tops(7)
                    values(6)
                if prv:
                    dve.wait_ge(S["ex"], u)
                    dve.sem_inc(passed, 1)
                    dve.max(ex_top[:, :], ex[:, :]).then_inc(S["ex_top"], 1)
                    dve.wait_ge(S["ex_top"], u)
                    dve.sem_inc(passed, 1)
                    dve.max_index(ex_at[:, :], ex_top[:, :], ex[:, :]).then_inc(S["ex_at"], 1)
                    dve.reciprocal(gate[o][:, :], ex_sum[:, :]).then_inc(S["gate"], 1)
                if nxt:
                    low_part(q_lo[o], q_hi[o], b_q, "q_hi", "q_lo", u)
                if cur:
                    values(7)
                if nxt:
                    low_part(k_lo[o], k_hi[o], b_k, "k_hi", "k_lo", u)
                    for hf in (0, 1):
                        dve.wait_ge(S["v_ps"], 2 * (u + 1) + hf + 1)
                        dve.tensor_tensor(val[o][:, 4 * hf:4 * hf + 4, :],
                                          ps_f[hf][:, :].rearrange("p (a d) -> p a d", a=4),
                                          b_v[:, :].unsqueeze(1).to_broadcast([P, 4, P]),
                                          ALU.add).then_inc(S["v_sb"], 1)
                if prv:
                    for hf in (0, 1):
                        dve.wait_ge(S["y_ps"], 2 * (u - 1) + hf + 1)
                        dve.tensor_tensor(y1[:, hf * 512:(hf + 1) * 512].rearrange("p (a d) -> p a d", a=4),
                                          ps_f[hf][:, :].rearrange("p (a d) -> p a d", a=4),
                                          be[o][:, :].unsqueeze(1).to_broadcast([P, 4, P]),
                                          ALU.add).then_inc(S["y1"], 1)
                    dve.wait_ge(S["gate"], u)
                    if above_zero(32 * (half + g - 1)):
                        dve.wait_ge(o_st[o], 32 * (half + g - 1))
                    for hf in (0, 1):
                        dve.wait_ge(S["y1"], 2 * (u - 1) + hf + 1)
                        dve.scalar_tensor_tensor(o_sb[o][:, 4 * hf:4 * hf + 4, :].rearrange("p a d -> p (a d)"),
                                                 y1[:, hf * 512:(hf + 1) * 512], gate[o][:, 0:1],
                                                 h3c[:, 4 * hf:4 * hf + 4, :].rearrange("p a d -> p (a d)"),
                                                 ALU.mult, ALU.add).then_inc(S["out"], 1)
            pipeline(dve, -1, B, 2, PAIRS, step)


_INS = ["x", "L0_tok_W", "L0_attn_W_Q", "L0_attn_W_K", "L0_attn_W_V", "L0_attn_W_G", "L0_attn_W_O",
        "L0_attn_gn_weight", "L0_attn_gn_bias", "L0_ffn_w_gating", "L0_ffn_gamma", "L0_ffn_w1",
        "L0_ffn_w2", "L1_attn_Wq", "L1_attn_bq", "L1_attn_Wk", "L1_attn_bk", "L1_attn_Wv",
        "L1_attn_bv", "L1_ffn_Wg", "L1_ffn_bg", "L1_ffn_We", "L1_ffn_be"]


def kernel(**inputs):
    import concourse.bacc as bacc
    from concourse.bass_utils import run_bass_kernel_spmd

    nc = bacc.Bacc("TRN2", target_bir_lowering=False, num_devices=1)
    arrays, t, cst = {}, {}, {}
    for name in _INS:
        a = np.ascontiguousarray(inputs[name])
        arrays["in_" + name] = a
        t[name] = nc.dram_tensor("in_" + name, a.shape, mybir.dt.from_np(a.dtype), kind="ExternalInput").ap()
    for name, a in constants().items():
        arrays["const_" + name] = a
        cst[name] = nc.dram_tensor("const_" + name, a.shape, mybir.dt.from_np(a.dtype), kind="ExternalInput").ap()
    out = nc.dram_tensor("out", (B, SEQ, P), F32, kind="ExternalOutput").ap()
    tower(nc, t, cst, out)
    r = run_bass_kernel_spmd(nc, [arrays], core_ids=[0])
    return r.results[0]["out"]
```
